# Optimizing a Trainium2 kernel written in Bass

```python
import numpy as np
import jax
import jax.numpy as jnp

def _softmax(x, axis=-1):
    return jax.nn.softmax(x, axis=axis)

def _gelu(x):
    return jax.nn.gelu(x, approximate=True)

def _silu(x):
    return jax.nn.silu(x)

def _sigmoid(x):
    return jax.nn.sigmoid(x)

def _layernorm(x, axis=-1, eps=1e-05):
    m = jnp.mean(x, axis=axis, keepdims=True)
    v = jnp.var(x, axis=axis, keepdims=True)
    return (x - m) / jnp.sqrt(v + eps)

def _scatter_add(tgt, idx, src, axis=0):
    return tgt.at[idx].add(src)

def _segment_sum(src, seg, n):
    return jax.ops.segment_sum(src, seg, n)
kernel_name = 'mk_dlrm_tower_d1_rec_r8_4abdee'

def setup_inputs(seed: int=0):
    np.random.seed(seed)
    _w = jnp.asarray

    def _rec_inputs():
        import jax
        import jax.numpy as jnp
        _tk = jax.random.key(seed)
        dense_ctx = jax.random.normal(jax.random.fold_in(_tk, 190), (1024, 16), jnp.float32)
        ids = jnp.stack([jax.random.randint(jax.random.fold_in(_tk, 200 + f), (1024,), 0, v, jnp.int32) for f, v in enumerate([125000, 1000, 1250, 12500, 1000, 12500, 125000, 1000, 125000, 125000, 12500, 12500, 1000, 125000, 1250, 1250, 12500, 125000, 125000, 1250, 1000, 12500, 125000, 1250, 12500, 125000, 12500, 1000, 1000, 125000, 1250, 12500, 125000, 1250, 1250, 12500, 1250, 1250, 125000])], axis=1)
        tbl_0 = 0.05 * jax.random.normal(jax.random.fold_in(_tk, 500 + 0), (125000, 16), jnp.float32)
        tbl_1 = 0.05 * jax.random.normal(jax.random.fold_in(_tk, 500 + 1), (1000, 16), jnp.float32)
        tbl_2 = 0.05 * jax.random.normal(jax.random.fold_in(_tk, 500 + 2), (1250, 16), jnp.float32)
        tbl_3 = 0.05 * jax.random.normal(jax.random.fold_in(_tk, 500 + 3), (12500, 16), jnp.float32)
        tbl_4 = 0.05 * jax.random.normal(jax.random.fold_in(_tk, 500 + 4), (1000, 16), jnp.float32)
        tbl_5 = 0.05 * jax.random.normal(jax.random.fold_in(_tk, 500 + 5), (12500, 16), jnp.float32)
        tbl_6 = 0.05 * jax.random.normal(jax.random.fold_in(_tk, 500 + 6), (125000, 16), jnp.float32)
        tbl_7 = 0.05 * jax.random.normal(jax.random.fold_in(_tk, 500 + 7), (1000, 16), jnp.float32)
        tbl_8 = 0.05 * jax.random.normal(jax.random.fold_in(_tk, 500 + 8), (125000, 16), jnp.float32)
        tbl_9 = 0.05 * jax.random.normal(jax.random.fold_in(_tk, 500 + 9), (125000, 16), jnp.float32)
        tbl_10 = 0.05 * jax.random.normal(jax.random.fold_in(_tk, 500 + 10), (12500, 16), jnp.float32)
        tbl_11 = 0.05 * jax.random.normal(jax.random.fold_in(_tk, 500 + 11), (12500, 16), jnp.float32)
        tbl_12 = 0.05 * jax.random.normal(jax.random.fold_in(_tk, 500 + 12), (1000, 16), jnp.float32)
        tbl_13 = 0.05 * jax.random.normal(jax.random.fold_in(_tk, 500 + 13), (125000, 16), jnp.float32)
        tbl_14 = 0.05 * jax.random.normal(jax.random.fold_in(_tk, 500 + 14), (1250, 16), jnp.float32)
        tbl_15 = 0.05 * jax.random.normal(jax.random.fold_in(_tk, 500 + 15), (1250, 16), jnp.float32)
        tbl_16 = 0.05 * jax.random.normal(jax.random.fold_in(_tk, 500 + 16), (12500, 16), jnp.float32)
        tbl_17 = 0.05 * jax.random.normal(jax.random.fold_in(_tk, 500 + 17), (125000, 16), jnp.float32)
        tbl_18 = 0.05 * jax.random.normal(jax.random.fold_in(_tk, 500 + 18), (125000, 16), jnp.float32)
        tbl_19 = 0.05 * jax.random.normal(jax.random.fold_in(_tk, 500 + 19), (1250, 16), jnp.float32)
        tbl_20 = 0.05 * jax.random.normal(jax.random.fold_in(_tk, 500 + 20), (1000, 16), jnp.float32)
        tbl_21 = 0.05 * jax.random.normal(jax.random.fold_in(_tk, 500 + 21), (12500, 16), jnp.float32)
        tbl_22 = 0.05 * jax.random.normal(jax.random.fold_in(_tk, 500 + 22), (125000, 16), jnp.float32)
        tbl_23 = 0.05 * jax.random.normal(jax.random.fold_in(_tk, 500 + 23), (1250, 16), jnp.float32)
        tbl_24 = 0.05 * jax.random.normal(jax.random.fold_in(_tk, 500 + 24), (12500, 16), jnp.float32)
        tbl_25 = 0.05 * jax.random.normal(jax.random.fold_in(_tk, 500 + 25), (125000, 16), jnp.float32)
        tbl_26 = 0.05 * jax.random.normal(jax.random.fold_in(_tk, 500 + 26), (12500, 16), jnp.float32)
        tbl_27 = 0.05 * jax.random.normal(jax.random.fold_in(_tk, 500 + 27), (1000, 16), jnp.float32)
        tbl_28 = 0.05 * jax.random.normal(jax.random.fold_in(_tk, 500 + 28), (1000, 16), jnp.float32)
        tbl_29 = 0.05 * jax.random.normal(jax.random.fold_in(_tk, 500 + 29), (125000, 16), jnp.float32)
        tbl_30 = 0.05 * jax.random.normal(jax.random.fold_in(_tk, 500 + 30), (1250, 16), jnp.float32)
        tbl_31 = 0.05 * jax.random.normal(jax.random.fold_in(_tk, 500 + 31), (12500, 16), jnp.float32)
        tbl_32 = 0.05 * jax.random.normal(jax.random.fold_in(_tk, 500 + 32), (125000, 16), jnp.float32)
        tbl_33 = 0.05 * jax.random.normal(jax.random.fold_in(_tk, 500 + 33), (1250, 16), jnp.float32)
        tbl_34 = 0.05 * jax.random.normal(jax.random.fold_in(_tk, 500 + 34), (1250, 16), jnp.float32)
        tbl_35 = 0.05 * jax.random.normal(jax.random.fold_in(_tk, 500 + 35), (12500, 16), jnp.float32)
        tbl_36 = 0.05 * jax.random.normal(jax.random.fold_in(_tk, 500 + 36), (1250, 16), jnp.float32)
        tbl_37 = 0.05 * jax.random.normal(jax.random.fold_in(_tk, 500 + 37), (1250, 16), jnp.float32)
        tbl_38 = 0.05 * jax.random.normal(jax.random.fold_in(_tk, 500 + 38), (125000, 16), jnp.float32)
        _rk = jax.random.fold_in(_tk, 7)
        W_top1 = 0.0606339 * jax.random.normal(jax.random.fold_in(_tk, 801), (272, 512), jnp.float32)
        W_top2 = 0.0441942 * jax.random.normal(jax.random.fold_in(_tk, 802), (512, 256), jnp.float32)
        W_top3 = 0.0625 * jax.random.normal(jax.random.fold_in(_tk, 803), (256, 1), jnp.float32)
        b_top1 = jnp.zeros((512,), jnp.float32)
        b_top2 = jnp.zeros((256,), jnp.float32)
        return (dense_ctx, ids, tbl_0, tbl_1, tbl_2, tbl_3, tbl_4, tbl_5, tbl_6, tbl_7, tbl_8, tbl_9, tbl_10, tbl_11, tbl_12, tbl_13, tbl_14, tbl_15, tbl_16, tbl_17, tbl_18, tbl_19, tbl_20, tbl_21, tbl_22, tbl_23, tbl_24, tbl_25, tbl_26, tbl_27, tbl_28, tbl_29, tbl_30, tbl_31, tbl_32, tbl_33, tbl_34, tbl_35, tbl_36, tbl_37, tbl_38, W_top1, b_top1, W_top2, b_top2, W_top3)
    dense_ctx, ids, tbl_0, tbl_1, tbl_2, tbl_3, tbl_4, tbl_5, tbl_6, tbl_7, tbl_8, tbl_9, tbl_10, tbl_11, tbl_12, tbl_13, tbl_14, tbl_15, tbl_16, tbl_17, tbl_18, tbl_19, tbl_20, tbl_21, tbl_22, tbl_23, tbl_24, tbl_25, tbl_26, tbl_27, tbl_28, tbl_29, tbl_30, tbl_31, tbl_32, tbl_33, tbl_34, tbl_35, tbl_36, tbl_37, tbl_38, W_top1, b_top1, W_top2, b_top2, W_top3 = _rec_inputs()

    def _L0_rec_setup():
        import jax, jax.numpy as jnp
        import numpy as np
        B, F, D = (1024, 39, 16)
        HIDDEN = [128, 128, 128]

        def _cin(x, Ws, bs):
            F0 = x.shape[1]
            h = x
            outs = []
            n = len(Ws)
            for i, (W, b) in enumerate(zip(Ws, bs)):
                L = W.shape[-1]
                Fk = h.shape[1]
                Wr = W.reshape(F0, Fk, L)
                z = jnp.einsum('bfd,bgd->bfgd', x, h)
                cur = jax.nn.relu(jnp.einsum('bfgd,fgl->bld', z, Wr) + b[None, :, None])
                if i != n - 1:
                    h = cur[:, :L // 2]
                    direct = cur[:, L // 2:]
                else:
                    direct = cur
                outs.append(direct)
            return jnp.concatenate(outs, axis=1).sum(-1)
        key = jax.random.key(seed)
        ks = jax.random.split(key, 8)
        x = jax.random.normal(ks[0], (B, F, D), dtype=jnp.float32)
        field_nums = [F]
        Ws, bs = ([], [])
        for i, L in enumerate(HIDDEN):
            fan_in = field_nums[0] * field_nums[-1]
            lim = np.sqrt(6.0 / fan_in)
            Ws.append(jax.random.uniform(ks[1 + i], (fan_in, L), jnp.float32, -lim, lim))
            bs.append(jnp.zeros((L,), jnp.float32))
            field_nums.append(L // 2)
        return {'x': x, 'W0': Ws[0], 'W1': Ws[1], 'W2': Ws[2], 'b0': bs[0], 'b1': bs[1], 'b2': bs[2]}
    _L0_rec_all = _L0_rec_setup()
    _L0_rec_in = {k: v for k, v in _L0_rec_all.items() if k in ('W0', 'W1', 'W2', 'b0', 'b1', 'b2')}
    del _L0_rec_all
    return {'dense_ctx': dense_ctx, 'ids': ids, 'tbl_0': tbl_0, 'tbl_1': tbl_1, 'tbl_2': tbl_2, 'tbl_3': tbl_3, 'tbl_4': tbl_4, 'tbl_5': tbl_5, 'tbl_6': tbl_6, 'tbl_7': tbl_7, 'tbl_8': tbl_8, 'tbl_9': tbl_9, 'tbl_10': tbl_10, 'tbl_11': tbl_11, 'tbl_12': tbl_12, 'tbl_13': tbl_13, 'tbl_14': tbl_14, 'tbl_15': tbl_15, 'tbl_16': tbl_16, 'tbl_17': tbl_17, 'tbl_18': tbl_18, 'tbl_19': tbl_19, 'tbl_20': tbl_20, 'tbl_21': tbl_21, 'tbl_22': tbl_22, 'tbl_23': tbl_23, 'tbl_24': tbl_24, 'tbl_25': tbl_25, 'tbl_26': tbl_26, 'tbl_27': tbl_27, 'tbl_28': tbl_28, 'tbl_29': tbl_29, 'tbl_30': tbl_30, 'tbl_31': tbl_31, 'tbl_32': tbl_32, 'tbl_33': tbl_33, 'tbl_34': tbl_34, 'tbl_35': tbl_35, 'tbl_36': tbl_36, 'tbl_37': tbl_37, 'tbl_38': tbl_38, 'W_top1': W_top1, 'b_top1': b_top1, 'W_top2': W_top2, 'b_top2': b_top2, 'W_top3': W_top3, 'L0_rec_W0': _L0_rec_in['W0'], 'L0_rec_W1': _L0_rec_in['W1'], 'L0_rec_W2': _L0_rec_in['W2'], 'L0_rec_b0': _L0_rec_in['b0'], 'L0_rec_b1': _L0_rec_in['b1'], 'L0_rec_b2': _L0_rec_in['b2']}

def reference(dense_ctx, ids, tbl_0, tbl_1, tbl_2, tbl_3, tbl_4, tbl_5, tbl_6, tbl_7, tbl_8, tbl_9, tbl_10, tbl_11, tbl_12, tbl_13, tbl_14, tbl_15, tbl_16, tbl_17, tbl_18, tbl_19, tbl_20, tbl_21, tbl_22, tbl_23, tbl_24, tbl_25, tbl_26, tbl_27, tbl_28, tbl_29, tbl_30, tbl_31, tbl_32, tbl_33, tbl_34, tbl_35, tbl_36, tbl_37, tbl_38, W_top1, b_top1, W_top2, b_top2, W_top3, L0_rec_W0, L0_rec_W1, L0_rec_W2, L0_rec_b0, L0_rec_b1, L0_rec_b2):
    import jax
    import jax.numpy as jnp

    def _L0_rec_ref(x, W0, W1, W2, b0, b1, b2):
        import jax, jax.numpy as jnp
        import numpy as np
        B, F, D = (1024, 39, 16)
        HIDDEN = [128, 128, 128]

        def _cin(x, Ws, bs):
            F0 = x.shape[1]
            h = x
            outs = []
            n = len(Ws)
            for i, (W, b) in enumerate(zip(Ws, bs)):
                L = W.shape[-1]
                Fk = h.shape[1]
                Wr = W.reshape(F0, Fk, L)
                z = jnp.einsum('bfd,bgd->bfgd', x, h)
                cur = jax.nn.relu(jnp.einsum('bfgd,fgl->bld', z, Wr) + b[None, :, None])
                if i != n - 1:
                    h = cur[:, :L // 2]
                    direct = cur[:, L // 2:]
                else:
                    direct = cur
                outs.append(direct)
            return jnp.concatenate(outs, axis=1).sum(-1)
        return _cin(x, [W0, W1, W2], [b0, b1, b2])
    e = jnp.stack([tbl_0[ids[:, 0]], tbl_1[ids[:, 1]], tbl_2[ids[:, 2]], tbl_3[ids[:, 3]], tbl_4[ids[:, 4]], tbl_5[ids[:, 5]], tbl_6[ids[:, 6]], tbl_7[ids[:, 7]], tbl_8[ids[:, 8]], tbl_9[ids[:, 9]], tbl_10[ids[:, 10]], tbl_11[ids[:, 11]], tbl_12[ids[:, 12]], tbl_13[ids[:, 13]], tbl_14[ids[:, 14]], tbl_15[ids[:, 15]], tbl_16[ids[:, 16]], tbl_17[ids[:, 17]], tbl_18[ids[:, 18]], tbl_19[ids[:, 19]], tbl_20[ids[:, 20]], tbl_21[ids[:, 21]], tbl_22[ids[:, 22]], tbl_23[ids[:, 23]], tbl_24[ids[:, 24]], tbl_25[ids[:, 25]], tbl_26[ids[:, 26]], tbl_27[ids[:, 27]], tbl_28[ids[:, 28]], tbl_29[ids[:, 29]], tbl_30[ids[:, 30]], tbl_31[ids[:, 31]], tbl_32[ids[:, 32]], tbl_33[ids[:, 33]], tbl_34[ids[:, 34]], tbl_35[ids[:, 35]], tbl_36[ids[:, 36]], tbl_37[ids[:, 37]], tbl_38[ids[:, 38]]], axis=1)
    z = _L0_rec_ref(e, L0_rec_W0, L0_rec_W1, L0_rec_W2, L0_rec_b0, L0_rec_b1, L0_rec_b2)
    z = z.reshape(z.shape[0], -1)
    h = jnp.concatenate([z, dense_ctx], axis=1)
    h = jnp.maximum(h @ W_top1 + b_top1, 0.0)
    h = jnp.maximum(h @ W_top2 + b_top2, 0.0)
    y = h @ W_top3
    return y

_drawn_inputs = setup_inputs


def setup_inputs(seed=0):
    import zlib

    import numpy as np

    out = dict(_drawn_inputs(seed))
    spreads = {'b_top1': (0.0, 2.0),
     'b_top2': (0.0, 2.0),
     'L0_rec_b0': (0.0, 0.333),
     'L0_rec_b1': (0.0, 0.48),
     'L0_rec_b2': (0.0, 0.8)}
    factors = {'tbl_0': 8.0,
     'tbl_1': 8.0,
     'tbl_2': 8.0,
     'tbl_3': 8.0,
     'tbl_4': 8.0,
     'tbl_5': 8.0,
     'tbl_6': 8.0,
     'tbl_7': 8.0,
     'tbl_8': 8.0,
     'tbl_9': 8.0,
     'tbl_10': 8.0,
     'tbl_11': 8.0,
     'tbl_12': 8.0,
     'tbl_13': 8.0,
     'tbl_14': 8.0,
     'tbl_15': 8.0,
     'tbl_16': 8.0,
     'tbl_17': 8.0,
     'tbl_18': 8.0,
     'tbl_19': 8.0,
     'tbl_20': 8.0,
     'tbl_21': 8.0,
     'tbl_22': 8.0,
     'tbl_23': 8.0,
     'tbl_24': 8.0,
     'tbl_25': 8.0,
     'tbl_26': 8.0,
     'tbl_27': 8.0,
     'tbl_28': 8.0,
     'tbl_29': 8.0,
     'tbl_30': 8.0,
     'tbl_31': 8.0,
     'tbl_32': 8.0,
     'tbl_33': 8.0,
     'tbl_34': 8.0,
     'tbl_35': 8.0,
     'tbl_36': 8.0,
     'tbl_37': 8.0,
     'tbl_38': 8.0,
     'L0_rec_W0': 8.0,
     'L0_rec_W1': 5.651,
     'L0_rec_W2': 4.837,
     'dense_ctx': 8.0}
    for name, (base, spread) in spreads.items():
        noise = np.random.default_rng([zlib.crc32(name.encode()), seed]).standard_normal(out[name].shape)
        drawn = base * np.exp(spread * noise) if base else spread * noise
        out[name] = jnp.asarray(drawn.astype(out[name].dtype))
    for name, factor in factors.items():
        out[name] = (out[name] * factor).astype(out[name].dtype)
    return out
```

```python
from contextlib import ExitStack

import concourse.bass as bass
from concourse import mybir

F32 = mybir.dt.float32
I32 = mybir.dt.int32
U32 = mybir.dt.uint32
ALU = mybir.AluOpType
ACT = mybir.ActivationFunctionType
AX = mybir.AxisListType

P = 128
B, F, D, L = 1024, 39, 16, 128
H = L // 2
NB = B // P
HD = D // 2
N = HD * P
BK = 512
NBK = N // BK
NST = 2 * NB
K = 3
SH = (F + 1) // 2
T0 = -(-SH // K)
R0 = K * F
XR = F + T0 * K - 1
T1 = -(-F // 2)
RING = 5
DN = 16
M1, M2 = 512, 256

HEAD = T0 + T1
ROUND = T0 + 2 * T1
PAIR = 2 * ROUND


def slot(i):
    return i % RING if i >= 0 else (PAIR + i) % RING


def before(i):
    m = i - 1
    while slot(m) != slot(i):
        m -= 1
    return m


def cin_tower(nc, dense, ids, tables, w_top1, b_top1, w_top2, b_top2, w_top3, w0, w1, w2, b0, b1, b2, out):
    xT = nc.dram_tensor("xT", [NB, 2, XR, N], F32, kind="Internal").ap()
    w0_cols = nc.dram_tensor("w0_cols", [F, XR, L], F32, kind="Internal").ap()
    w0_rows = nc.dram_tensor("w0_rows", [XR, F, L], F32, kind="Internal").ap()

    with ExitStack() as ctx:
        def sb(name, shape, dt=F32):
            return ctx.enter_context(nc.sbuf_tensor(name, shape, dt))

        def sem(name):
            return ctx.enter_context(nc.semaphore(name))

        ps = [ctx.enter_context(nc.psum_tensor(n, [P, N], F32)) for n in ("cur0", "cur1", "cur2", "spare")]
        cur0, cur1, cur2, spare = ps

        ident = sb("ident", [P, P])
        idx = sb("idx", [P, F], I32)
        emb = sb("emb", [P, F * D])
        xc = sb("xc", [F, 2, N])
        xk = sb("xk", [R0, N])
        xs = sb("xs", [R0, T0, N])
        xr = sb("xr", [P, T1, N])
        z = sb("z", [P, RING, N])
        h1 = sb("h1", [P, N])
        h2 = sb("h2", [P, N])
        direct = sb("direct", [P, N])
        last = sb("last", [P, N])
        w0s = sb("w0s", [P, T0, L])
        w1s = sb("w1s", [P, T1, L])
        w2s = sb("w2s", [P, T1, L])
        bias0 = sb("bias0", [P, 1])
        bias1 = sb("bias1", [P, 1])
        bias2 = sb("bias2", [P, 1])
        zA = sb("zA", [P, B])
        zB = sb("zB", [P, B])
        zC = sb("zC", [DN, B])
        sumA = sb("sumA", [P, P])
        sumB = sb("sumB", [P, P])
        w0t = z[:, 0, 0:T0 * L].rearrange("p (t l) -> p t l", t=T0)
        dn = z[:, 1, 0:NB * DN].rearrange("p (j c) -> p j c", j=NB)

        hid1 = xr[:, 0:M1 // P, :]
        hid2 = xr[:, 4:4 + M2 // P, :]
        y = xr[0:1, 6, :]
        wA = sb("wA", [P, M1])
        wB = sb("wB", [P, M1])
        wC = sb("wC", [DN, M1])
        wt2 = sb("wt2", [P, M1 // P, M2])
        wt3 = sb("wt3", [P, M2 // P])
        bt1 = sb("bt1", [P, M1 // P])
        bt2 = sb("bt2", [P, M2 // P])

        ident_zeroed = sem("ident_zeroed")
        ident_ready = sem("ident_ready")
        idx_loaded = sem("idx_loaded")
        gathered = sem("gathered")
        small_loaded = sem("small_loaded")
        weights_loaded = sem("weights_loaded")
        w0_copied = sem("w0_copied")
        w0_zeroed = sem("w0_zeroed")
        w0_loaded = sem("w0_loaded")
        w0_ready = sem("w0_ready")
        transposed = sem("transposed")
        xc_copied = sem("xc_copied")
        xT_written = sem("xT_written")
        xs_loaded = sem("xs_loaded")
        xr_loaded = [sem(f"xr_loaded{q}") for q in range(T1 // 2)]
        z_ready = sem("z_ready")
        z_used = sem("z_used")
        evac0 = sem("evac0")
        evac1 = sem("evac1")
        evac2 = sem("evac2")
        sum_done = sem("sum_done")
        add_done = sem("add_done")
        dense_turned = sem("dense_turned")
        dense_copied = sem("dense_copied")
        top_done = sem("top_done")
        top_read = sem("top_read")
        out_written = sem("out_written")

        block = ctx.enter_context(nc.Block())

        def first_tile(j):
            return HEAD + PAIR * j

        @block.gpsimd
        def _(pool):
            nc.gpsimd.memset(ident[:], 1.0).then_inc(ident_zeroed, 1)
            pool.wait_ge(ident_zeroed, 1)
            nc.gpsimd.affine_select(out=ident[:], in_=ident[:], compare_op=ALU.is_equal, fill=0.0, base=0,
                                    pattern=[[-1, P]], channel_multiplier=1).then_inc(ident_ready, 1)

            def gather(j):
                pool.dma_start(idx[:, :], ids[bass.ds(j * P, P), :]).then_inc(idx_loaded, 16)
                pool.wait_ge(idx_loaded, 16 * (j + 1))
                pool.nop(nofuse=True)
                for f in range(F):
                    nc.gpsimd.indirect_dma_start(
                        out=emb[:, f * D:(f + 1) * D], out_offset=None, in_=tables[f],
                        in_offset=bass.IndirectOffsetOnAxis(ap=idx[:, f:f + 1].bitcast(U32), axis=0),
                    ).then_inc(gathered, 16)

            gather(0)
            with pool.Fori(1, NB) as j:
                pool.wait_ge(gathered, 16 * F * j)
                pool.wait_ge(transposed, 4 * j)
                gather(j)

        @block.sync
        def _(sp):
            w0v = w0.rearrange("(f g) l -> f g l", f=F)
            sp.dma_start(w0_cols[:, 0:F, :], w0v).then_inc(w0_copied, 16)
            sp.dma_start(w0_cols[:, F:XR, :], w0v[:, 0:XR - F, :]).then_inc(w0_copied, 16)
            sp.dma_start(w0_rows[0:F, :, :], w0v).then_inc(w0_copied, 16)
            sp.dma_start(w0_rows[F:XR, :, :], w0v[0:XR - F, :, :]).then_inc(w0_copied, 16)
            with nc.allow_non_contiguous_dma(reason="a few small columns"):
                sp.dma_start(bias0[:, :], b0.rearrange("(l o) -> l o", o=1)).then_inc(small_loaded, 16)
                b1v = b1.rearrange("(l o) -> l o", o=1)
                sp.dma_start(bias1[0:H, :], b1v[H:L, :]).then_inc(small_loaded, 16)
                sp.dma_start(bias1[H:L, :], b1v[0:H, :]).then_inc(small_loaded, 16)
                sp.dma_start(bias2[:, :], b2.rearrange("(l o) -> l o", o=1)).then_inc(small_loaded, 16)
                sp.dma_start(bt1[:, :], b_top1.rearrange("(m p) -> p m", p=P)).then_inc(small_loaded, 16)
                sp.dma_start(bt2[:, :], b_top2.rearrange("(m p) -> p m", p=P)).then_inc(small_loaded, 16)
                sp.dma_start(wt3[:, :], w_top3.rearrange("(m p) o -> p (m o)", p=P)).then_inc(small_loaded, 16)
                sp.dma_start(dn, dense.rearrange("(j p) c -> p j c", p=P)).then_inc(small_loaded, 16)
            sp.wait_ge(w0_copied, 64)
            sp.wait_ge(w0_zeroed, 2)
            for t in range(T0):
                for k in range(K):
                    s = K * t + k
                    if s < SH:
                        cols = bass.AP(w0_cols.tensor, s * L, [[(XR + 1) * L, F], [1, L]])
                        sp.dma_start(w0s[k:R0:K, t, :], cols).then_inc(w0_loaded, 16)
                    if 0 < s < SH:
                        rows = bass.AP(w0_rows.tensor, s * F * L, [[(F + 1) * L, F], [1, L]])
                        sp.dma_start(w0t[k:R0:K, t, :], rows).then_inc(w0_loaded, 16)
            full = P * (T1 - 1)
            for w, ws, cols in ((w1, w1s, ((0, H, H), (H, 0, H))), (w2, w2s, ((0, 0, L),))):
                for to, fr, n in cols:
                    sp.dma_start(ws[:, 0:T1 - 1, to:to + n],
                                 w[0:full, fr:fr + n].rearrange("(t p) l -> p t l", p=P)).then_inc(weights_loaded, 16)
                    sp.dma_start(ws[0:H, T1 - 1, to:to + n],
                                 w[full:full + H, fr:fr + n]).then_inc(weights_loaded, 16)

            def load_xs(j, half):
                for k in range(K):
                    src = bass.AP(xT.tensor, (2 * j + half) * XR * N + k * N, [[N, F], [K * N, T0], [1, N]])
                    sp.dma_start(xs[k:R0:K, :, :], src).then_inc(xs_loaded, 16)
                    src = bass.AP(xT.tensor, (2 * j + half) * XR * N, [[N, F], [1, N]])
                    sp.dma_start(xk[k:R0:K, :], src).then_inc(xs_loaded, 16)

            def load_xr(q, j, half):
                for par in range(2):
                    n = 2 if 4 * q + 2 + par < F else 1
                    src = bass.AP(xT.tensor, (2 * j + half) * XR * N + (4 * q + par) * N,
                                  [[0, H], [2 * N, n], [1, N]])
                    sp.dma_start(xr[par * H:par * H + H, 2 * q:2 * q + n, :], src).then_inc(xr_loaded[q], 16)

            def round_loads(s, base, j_next, half_next):
                sp.wait_ge(xT_written, 32 * (j_next + 1))
                sp.wait_ge(z_ready, base - T1)
                load_xs(j_next, half_next)
                for q in range(T1 // 2):
                    sp.wait_ge(z_ready, base + T0 + 2 * q + 2)
                    load_xr(q, j_next, half_next)

            sp.wait_ge(xT_written, 32)
            load_xs(0, 0)
            for q in range(T1 // 2):
                load_xr(q, 0, 0)
            sp.dma_start(wA[0:H, :], w_top1[H:2 * H, :]).then_inc(small_loaded, 16)
            sp.dma_start(wA[H:P, :], w_top1[0:H, :]).then_inc(small_loaded, 16)
            sp.dma_start(wB[:, :], w_top1[P:2 * P, :]).then_inc(small_loaded, 16)
            sp.dma_start(wC[:, :], w_top1[2 * P:2 * P + DN, :]).then_inc(small_loaded, 16)
            sp.dma_start(wt2[:, :, :], w_top2.rearrange("(k p) n -> p k n", p=P)).then_inc(small_loaded, 16)
            with sp.Fori(0, NB - 1) as j:
                round_loads(2 * j, first_tile(j), j, 1)
                round_loads(2 * j + 1, first_tile(j) + ROUND, j + 1, 0)
            round_loads(NST - 2, first_tile(NB - 1), NB - 1, 1)
            sp.wait_ge(top_read, 14)
            sp.dma_start(out.rearrange("b o -> o b"), y).then_inc(out_written, 16)
            sp.wait_ge(out_written, 16)

        @block.vector
        def _(dve):
            nc.vector.memset(w0s[:], 0.0).then_inc(w0_zeroed, 1)
            nc.vector.memset(w0t, 0.0).then_inc(w0_zeroed, 1)
            dve.wait_ge(w0_loaded, 16 * (2 * SH - 1))
            nc.vector.tensor_tensor(w0s[:], w0s[:], w0t, ALU.add).then_inc(w0_ready, 1)

            def product(base, i, a, b, rows):
                dve.wait_ge(z_used, base + before(i) + 1)
                nc.vector.tensor_tensor(z[0:rows, slot(i), :], a, b, ALU.mult).then_inc(z_ready, 1)

            def layer0(base, i, s, half):
                dve.wait_ge(xs_loaded, 32 * K * (s + 1))
                for t in range(T0):
                    product(base, i + t, xk[:, :], xs[:, t, :], R0)

            def layer12(base, i, s, h):
                for t in range(T1):
                    if t % 2 == 0:
                        dve.wait_ge(xr_loaded[t // 2], 32 * (s + 1))
                    rows = P if 2 * t + 1 < F else H
                    product(base, i + t, xr[0:rows, t, :], h[0:rows, :], rows)

            def sum_d(src, s, half, j, which, total, part):
                dst = total[:, bass.ds(j * P, P)]
                nc.vector.tensor_reduce(part[:] if half else dst, src[:].rearrange("p (d b) -> p b d", d=HD),
                                        AX.X, ALU.add).then_inc(sum_done, 1)
                if half:
                    dve.wait_ge(sum_done, 2 * s + 1 + which)
                    nc.vector.tensor_tensor(dst, dst, part[:], ALU.add).then_inc(add_done, 1)

            def round_(s, base, i, j, half):
                layer0(base, i, s + 1, 1 - half)
                dve.wait_ge(evac1, 3 * (s + 1))
                sum_d(direct, s, half, j, 0, zA, sumA)
                layer12(base, i + T0, s, h2)
                dve.wait_ge(evac0, 3 * (s + 2))
                for t in range(T1):
                    if t == 8:
                        dve.wait_ge(evac2, s + 1)
                        sum_d(last, s, half, j, 1, zB, sumB)
                    if t % 2 == 0:
                        dve.wait_ge(xr_loaded[t // 2], 32 * (s + 2))
                    rows = P if 2 * t + 1 < F else H
                    product(base, i + T0 + T1 + t, xr[0:rows, t, :], h1[0:rows, :], rows)

            dve.wait_ge(dense_turned, 1)
            dve.wait_ge(w0_ready, 1)
            dve.wait_ge(xs_loaded, 32 * K)
            for t in range(HEAD):
                if t == T0:
                    dve.wait_ge(evac0, 3)
                if t >= RING:
                    dve.wait_ge(z_used, HEAD + before(t - HEAD) + 1)
                if t < T0:
                    nc.vector.tensor_tensor(z[0:R0, slot(t - HEAD), :], xk[:, :], xs[:, t, :],
                                            ALU.mult).then_inc(z_ready, 1)
                else:
                    u = t - T0
                    if u % 2 == 0:
                        dve.wait_ge(xr_loaded[u // 2], 32)
                    rows = P if 2 * u + 1 < F else H
                    nc.vector.tensor_tensor(z[0:rows, slot(t - HEAD), :], xr[0:rows, u, :], h1[0:rows, :],
                                            ALU.mult).then_inc(z_ready, 1)
            with dve.Fori(0, NB - 1) as j:
                round_(2 * j, first_tile(j), 0, j, 0)
                round_(2 * j + 1, first_tile(j), ROUND, j, 1)
            base = first_tile(NB - 1)
            round_(NST - 2, base, 0, NB - 1, 0)
            dve.wait_ge(evac1, 3 * NST)
            sum_d(direct, NST - 1, 1, NB - 1, 0, zA, sumA)
            layer12(base, ROUND, NST - 1, h2)
            dve.wait_ge(evac2, NST)
            sum_d(last, NST - 1, 1, NB - 1, 1, zB, sumB)

        @block.scalar
        def _(act):
            def copy_xc(j):
                if j is not 0:
                    act.wait_ge(xT_written, 32 * j)
                for r in range(4):
                    act.wait_ge(transposed, 4 * j + r + 1)
                    nc.scalar.activation(xc[:, r // 2, (r % 2) * BK:(r % 2 + 1) * BK],
                                         spare[0:F, (r % 2) * BK:(r % 2 + 1) * BK], ACT.Copy).then_inc(xc_copied, 1)
                act.wait_ge(xc_copied, 4 * (j + 1))
                to = [xT[bass.ds(j, 1), :, 0:F, :], xT[bass.ds(j, 1), :, F:XR, :]]
                act.dma_start(to[0].rearrange("o h f c -> (o f) h c"), xc[:, :, :]).then_inc(xT_written, 16)
                act.dma_start(to[1].rearrange("o h f c -> (o f) h c"),
                              xc[0:XR - F, :, :]).then_inc(xT_written, 16)

            def relu(dst, src, bias, done):
                nc.scalar.activation(dst, src, ACT.Relu, bias=bias).then_inc(done, 1)

            def read0(s, base_done):
                act.wait_ge(z_used, base_done)
                relu(h1[0:H, :], cur0[0:H, :], bias0[0:H, :], evac0)
                relu(h1[H:P, :], cur0[0:H, :], bias0[0:H, :], evac0)
                if s is not 0:
                    act.wait_ge(sum_done, 2 * s - 1)
                relu(direct[H:P, :], cur0[H:P, :], bias0[H:P, :], evac0)

            def read1(base_done):
                act.wait_ge(z_used, base_done)
                relu(h2[0:H, :], cur1[H:P, :], bias1[H:P, :], evac1)
                relu(h2[H:P, :], cur1[H:P, :], bias1[H:P, :], evac1)
                relu(direct[0:H, :], cur1[0:H, :], bias1[0:H, :], evac1)

            def read2(base_done):
                act.wait_ge(z_used, base_done)
                relu(last[:, :], cur2[:, :], bias2[:, :], evac2)

            act.wait_ge(dense_turned, 1)
            nc.scalar.activation(zC[:, :], spare[0:DN, :], ACT.Copy).then_inc(dense_copied, 1)
            copy_xc(0)
            act.wait_ge(small_loaded, 16 * 8)
            read0(0, T0)
            read1(HEAD)

            def round_(s, base, copy_next):
                read0(s + 1, base + T0)
                if copy_next is not None:
                    copy_xc(copy_next)
                read2(base + T0 + T1)
                read1(base + ROUND)

            with act.Fori(0, NB - 1) as j:
                round_(2 * j, first_tile(j), j + 1)
                round_(2 * j + 1, first_tile(j) + ROUND, None)
            round_(NST - 2, first_tile(NB - 1), None)
            read2(first_tile(NB - 1) + ROUND + T1)

            act.wait_ge(small_loaded, 16 * 13)
            g = 0
            for n in range(NBK):
                for m in range(M1 // P):
                    act.wait_ge(top_done, g + 1)
                    relu(hid1[:, m, n * BK:(n + 1) * BK], ps[g // 2][:, (g % 2) * BK:(g % 2 + 1) * BK],
                         bt1[:, m:m + 1], top_read)
                    g += 1
            for n in range(NBK):
                for m in range(M2 // P):
                    act.wait_ge(top_done, g + 1)
                    relu(hid2[:, m, n * BK:(n + 1) * BK], ps[(g % 8) // 2][:, (g % 2) * BK:(g % 2 + 1) * BK],
                         bt2[:, m:m + 1], top_read)
                    g += 1
            for n in range(NBK):
                act.wait_ge(top_done, g + 1)
                nc.scalar.activation(y[:, n * BK:(n + 1) * BK], ps[(g % 8) // 2][0:1, (g % 2) * BK:(g % 2 + 1) * BK],
                                     ACT.Copy).then_inc(top_read, 1)
                g += 1

        @block.tensor
        def _(pe):
            def transposes(j):
                pe.wait_ge(gathered, 16 * F * (j + 1))
                pe.nop(nofuse=True)
                ev = emb[:, :].rearrange("p (f d) -> p f d", d=D)
                for r in range(4):
                    if r >= 2:
                        pe.wait_ge(xc_copied, 4 * j + r - 1)
                        pe.nop(nofuse=True)
                    for c in range(4):
                        d = 4 * r + c
                        src = ev[:, :, d]
                        mm = nc.tensor.transpose(spare[0:F, (r % 2) * BK + c * P:(r % 2) * BK + (c + 1) * P],
                                                 src, ident[:, :])
                    mm.then_inc(transposed, 1)

            def contract(cur, w, base, i, tiles, rows_of):
                for t in range(tiles):
                    pe.wait_ge(z_ready, base + i + t + 1)
                    r = rows_of(t)
                    for b in range(NBK):
                        mm = nc.tensor.matmul(cur[:, b * BK:(b + 1) * BK], w[0:r, t, :],
                                              z[0:r, slot(i + t), b * BK:(b + 1) * BK],
                                              start=(t == 0), stop=(t == tiles - 1))
                    mm.then_inc(z_used, 1)

            def rows0(t):
                return R0

            def rows12(t):
                return P if 2 * t + 1 < F else H

            pe.wait_ge(ident_ready, 1)
            pe.wait_ge(small_loaded, 16 * 8)
            for c in range(NB):
                mm = nc.tensor.transpose(spare[0:DN, c * P:(c + 1) * P], dn[:, c, :], ident[:, :])
            mm.then_inc(dense_turned, 1)
            pe.wait_ge(dense_copied, 1)
            transposes(0)
            pe.wait_ge(w0_ready, 1)
            contract(cur0, w0s, HEAD, -HEAD, T0, rows0)
            pe.wait_ge(weights_loaded, 16 * 6)
            contract(cur1, w1s, HEAD, -T1, T1, rows12)

            def round_(s, base, i, copy_next):
                pe.wait_ge(evac0, 3 * (s + 1))
                contract(cur0, w0s, base, i, T0, rows0)
                if copy_next is not None:
                    transposes(copy_next)
                if s is not 0:
                    pe.wait_ge(evac2, s)
                contract(cur2, w2s, base, i + T0, T1, rows12)
                pe.wait_ge(evac1, 3 * (s + 1))
                contract(cur1, w1s, base, i + T0 + T1, T1, rows12)

            with pe.Fori(0, NB - 1) as j:
                round_(2 * j, first_tile(j), 0, j + 1)
                round_(2 * j + 1, first_tile(j), ROUND, None)
            round_(NST - 2, first_tile(NB - 1), 0, None)
            pe.wait_ge(evac2, NST - 1)
            contract(cur2, w2s, first_tile(NB - 1), ROUND, T1, rows12)

            pe.wait_ge(small_loaded, 16 * 13)
            pe.wait_ge(evac0, 3 * NST)
            pe.wait_ge(evac1, 3 * NST)
            pe.wait_ge(evac2, NST)
            pe.wait_ge(add_done, 2 * NB)
            g = 0

            def bank(g):
                return ps[(g % 8) // 2][:, (g % 2) * BK:(g % 2 + 1) * BK]

            for n in range(NBK):
                for m in range(M1 // P):
                    parts = ((wA, zA), (wB, zB), (wC, zC))
                    for q, (w, v) in enumerate(parts):
                        mm = nc.tensor.matmul(bank(g), w[:, m * P:(m + 1) * P], v[:, n * BK:(n + 1) * BK],
                                              start=(q == 0), stop=(q == len(parts) - 1))
                    mm.then_inc(top_done, 1)
                    g += 1
            for n in range(NBK):
                pe.wait_ge(top_read, (n + 1) * (M1 // P))
                for m in range(M2 // P):
                    if g - 8 >= (n + 1) * (M1 // P):
                        pe.wait_ge(top_read, g - 7)
                    for q in range(M1 // P):
                        mm = nc.tensor.matmul(bank(g), wt2[:, q, m * P:(m + 1) * P], hid1[:, q, n * BK:(n + 1) * BK],
                                              start=(q == 0), stop=(q == M1 // P - 1))
                    mm.then_inc(top_done, 1)
                    g += 1
            for n in range(NBK):
                pe.wait_ge(top_read, NBK * M1 // P + (n + 1) * (M2 // P))
                for q in range(M2 // P):
                    mm = nc.tensor.matmul(bank(g)[0:1, :], wt3[:, q:q + 1], hid2[:, q, n * BK:(n + 1) * BK],
                                          start=(q == 0), stop=(q == M2 // P - 1))
                mm.then_inc(top_done, 1)
                g += 1


_TBL = [f"tbl_{f}" for f in range(F)]
_INS = (["dense_ctx", "ids"] + _TBL + ["W_top1", "b_top1", "W_top2", "b_top2", "W_top3"]
        + ["L0_rec_W0", "L0_rec_W1", "L0_rec_W2", "L0_rec_b0", "L0_rec_b1", "L0_rec_b2"])


def kernel(**inputs):
    import numpy as _np
    import concourse.bacc as _bacc
    from concourse import mybir as _mybir
    from concourse.bass_utils import run_bass_kernel_spmd as _run

    nc = _bacc.Bacc("TRN2", target_bir_lowering=False, num_devices=1)
    arrays, aps = {}, {}
    for name in _INS:
        a = _np.ascontiguousarray(inputs[name])
        arrays[f"in_{name}_dram"] = a
        aps[name] = nc.dram_tensor(f"in_{name}_dram", a.shape, _mybir.dt.from_np(a.dtype), kind="ExternalInput").ap()
    out = nc.dram_tensor("out_0_dram", (B, 1), F32, kind="ExternalOutput").ap()
    args = [aps["dense_ctx"], aps["ids"], [aps[n] for n in _TBL]] + [aps[n] for n in _INS[2 + F:]]
    cin_tower(nc, *args, out)
    r = _run(nc, [arrays], core_ids=[0])
    return r.results[0]["out_0_dram"]
```

```python
from contextlib import ExitStack

import concourse.bass as bass
from concourse import mybir

F32 = mybir.dt.float32
I32 = mybir.dt.int32
U32 = mybir.dt.uint32
ALU = mybir.AluOpType
ACT = mybir.ActivationFunctionType
AX = mybir.AxisListType

P = 128
B, F, D, L = 1024, 39, 16, 128
H = L // 2
NB = B // P
HD = D // 2
N = HD * P
BK = 512
NBK = N // BK
NST = 2 * NB
K = 3
SH = (F + 1) // 2
T0 = -(-SH // K)
R0 = K * F
XR = F + T0 * K - 1
T1 = -(-F // 2)
DN = 16
M1, M2 = 512, 256
F32R = mybir.dt.float32r

KINDS0 = "FDFGFDF"
KINDS1 = "GFDFGFGFDFGFGDFGFDGF"
KINDS = {0: KINDS0, 1: KINDS1, 2: KINDS1}

ROUND = T0 + 2 * T1
PAIR = 2 * ROUND
HEAD = T0 + T1
ROUND_KINDS = KINDS[0] + KINDS[2] + KINDS[1]
HEAD_KINDS = KINDS[0] + KINDS[1]
PAIR_KINDS = ROUND_KINDS + ROUND_KINDS
LAST_KINDS = ROUND_KINDS + KINDS[2]
RING = 5
SPLIT_RING = 4
XS_RING = 4
LAG_SUB = 2
LAG_READ = 3


def kind(kinds, i):
    return kinds[i] if i >= 0 else HEAD_KINDS[i + HEAD]


def splits(kinds, i, which="DG"):
    if i >= 0:
        return sum(k in which for k in kinds[:i + 1])
    return -sum(k in which for k in HEAD_KINDS[i + 1 + HEAD:])


def total(which, j):
    return sum(k in which for k in HEAD_KINDS) + j * sum(k in which for k in PAIR_KINDS)


def slot(i):
    return i % RING if i >= 0 else (PAIR + i) % RING


def split_slot(kinds, i):
    n = splits(kinds, i) - 1
    return n % SPLIT_RING if n >= 0 else (splits(PAIR_KINDS, PAIR - 1) + n) % SPLIT_RING


def before(i):
    m = i - 1
    while slot(m) != slot(i):
        m -= 1
    return m


def split_before(kinds, i):
    m = i - 1
    while m >= -HEAD and (kind(kinds, m) == "F" or split_slot(kinds, m) != split_slot(kinds, i)):
        m -= 1
    return m if m >= -HEAD else None


def start(j):
    return HEAD + PAIR * j


def rows1(t):
    return P if 2 * t + 1 < F else H


def which_tile(kinds, i):
    if i < 0:
        i += HEAD
        return (0, i) if i < T0 else (1, i - T0)
    if kinds is LAST_KINDS and i >= ROUND:
        return 2, i - ROUND
    i %= ROUND
    return (0, i) if i < T0 else (2, i - T0) if i < T0 + T1 else (1, i - T0 - T1)


def cin_tower(nc, dense, ids, tables, w_top1, b_top1, w_top2, b_top2, w_top3, w0, w1, w2, b0, b1, b2, out):
    xT = nc.dram_tensor("xT", [NB, 2, XR, N], F32, kind="Internal").ap()
    w0_cols = nc.dram_tensor("w0_cols", [F, XR, L], F32, kind="Internal").ap()
    w0_rows = nc.dram_tensor("w0_rows", [XR, F, L], F32, kind="Internal").ap()

    with ExitStack() as ctx:
        def sb(name, shape, dt=F32):
            return ctx.enter_context(nc.sbuf_tensor(name, shape, dt))

        def sem(name):
            return ctx.enter_context(nc.semaphore(name))

        curA, curB, h1, h2 = [ctx.enter_context(nc.psum_tensor(n, [P, N], F32)) for n in ("curA", "curB", "h1", "h2")]

        ident = sb("ident", [P, P])
        idx = sb("idx", [P, F], I32)
        emb = sb("emb", [P, F * D])
        xk = sb("xk", [R0, N])
        xs = sb("xs", [R0, XS_RING, N])
        xr = sb("xr", [P, T1, N])
        z = sb("z", [P, RING, N])
        zh = sb("zh", [P, SPLIT_RING, N], F32R)
        zl = sb("zl", [P, SPLIT_RING, N], F32R)
        direct = sb("direct", [P, N])
        last = sb("last", [P, N])
        xc = last[0:F, :]
        zA = sb("zA", [P, B])
        zB = sb("zB", [P, B])
        part = sb("part", [P, P])
        bias0 = sb("bias0", [P, 1])
        bias1 = sb("bias1", [P, 1])
        bias2 = sb("bias2", [P, 1])
        bt1 = sb("bt1", [P, M1 // P])
        bt2 = sb("bt2", [P, M2 // P])
        wt3 = sb("wt3", [P, M2 // P])
        wf = {n: sb(f"wf{n}", [P, KINDS[n].count("F"), L]) for n in KINDS}
        wh = {n: sb(f"wh{n}", [P, len(KINDS[n]) - KINDS[n].count("F"), L], F32R) for n in KINDS}
        wl = {n: sb(f"wl{n}", [P, len(KINDS[n]) - KINDS[n].count("F"), L], F32R) for n in KINDS}

        def full_at(n, t):
            return KINDS[n][:t].count("F")

        def split_at(n, t):
            return t - full_at(n, t)

        per = N // L
        stage = {0: xr[:, 0:1, :].rearrange("p a (t l) -> p (a t) l", l=L)[:, 0:T0, :],
                 1: xr[:, 2:2 + -(-T1 // per), :].rearrange("p a (t l) -> p (a t) l", l=L)[:, 0:T1, :],
                 2: xr[:, 5:5 + -(-T1 // per), :].rearrange("p a (t l) -> p (a t) l", l=L)[:, 0:T1, :]}
        w0t = xr[:, 1:2, :].rearrange("p a (t l) -> p (a t) l", l=L)[:, 0:T0, :]
        emb1 = zB[:, 0:F * D]

        hid1 = xr[:, 0:M1 // P, :]
        hid2 = xr[:, 4:4 + M2 // P, :]
        y = xr[0:1, 6, :]
        wA = xr[:, 7, 0:M1]
        wB = xr[:, 7, M1:2 * M1]
        wC = xr[0:DN, 8, 0:M1]
        wt2 = xr[:, 9, :].rearrange("p (k n) -> p k n", n=M2)
        zC = xr[0:DN, 10, :]
        dn = xr[:, 8, M1:M1 + NB * DN].rearrange("p (j c) -> p j c", c=DN)
        TOP_SLOTS = 11

        ident_zeroed = sem("ident_zeroed")
        ident_ready = sem("ident_ready")
        idx_loaded = sem("idx_loaded")
        gathered = sem("gathered")
        emb_copied = sem("emb_copied")
        small_loaded = sem("small_loaded")
        weights_loaded = sem("weights_loaded")
        w0_copied = sem("w0_copied")
        w0_zeroed = sem("w0_zeroed")
        w0_loaded = sem("w0_loaded")
        w0_summed = sem("w0_summed")
        w_hi = sem("w_hi")
        w_lo = sem("w_lo")
        transposed = sem("transposed")
        xc_copied = sem("xc_copied")
        xT_written = [sem(f"xT_written{h}") for h in range(2)]
        xk_loaded = sem("xk_loaded")
        xs_loaded = [sem(f"xs_loaded{r}") for r in range(XS_RING)]
        xr_loaded = [sem(f"xr_loaded{q}") for q in range(T1 // 2)]
        z_ready = sem("z_ready")
        hi_ready = sem("hi_ready")
        lo_dve = sem("lo_dve")
        lo_pool = sem("lo_pool")
        z_used = sem("z_used")
        read0 = sem("read0")
        read1 = sem("read1")
        read2 = sem("read2")
        sum_done = sem("sum_done")
        add_done = sem("add_done")
        top_loaded = sem("top_loaded")
        dense_loaded = sem("dense_loaded")
        dense_turned = sem("dense_turned")
        dense_copied = sem("dense_copied")
        top_done = sem("top_done")
        top_read = sem("top_read")
        out_written = sem("out_written")

        block = ctx.enter_context(nc.Block())

        @block.gpsimd
        def _(pool):
            def load_ids(b):
                pool.dma_start(idx[:, :], ids[bass.ds(b * P, P), :]).then_inc(idx_loaded, 16)

            def gather(f, to):
                nc.gpsimd.indirect_dma_start(
                    out=to[:, f * D:(f + 1) * D], out_offset=None, in_=tables[f],
                    in_offset=bass.IndirectOffsetOnAxis(ap=idx[:, f:f + 1].bitcast(U32), axis=0),
                ).then_inc(gathered, 16)

            def subtract(kinds, j, i):
                if kind(kinds, i) == "G":
                    n, t = which_tile(kinds, i)
                    r = R0 if n == 0 else rows1(t)
                    q = split_slot(kinds, i)
                    pool.wait_ge(hi_ready, total("DG", j) + splits(kinds, i))
                    nc.gpsimd.tensor_tensor(zl[0:r, q, :], z[0:r, slot(i), :], zh[0:r, q, :],
                                            ALU.subtract).then_inc(lo_pool, 1)

            load_ids(0)
            nc.gpsimd.memset(ident[:], 1.0).then_inc(ident_zeroed, 1)
            pool.wait_ge(idx_loaded, 16)
            for f in range(F):
                gather(f, emb)
            pool.wait_ge(ident_zeroed, 1)
            nc.gpsimd.affine_select(out=ident[:], in_=ident[:], compare_op=ALU.is_equal, fill=0.0, base=0,
                                    pattern=[[-1, P]], channel_multiplier=1).then_inc(ident_ready, 1)
            pool.wait_ge(gathered, 16 * F)
            load_ids(1)
            pool.wait_ge(idx_loaded, 32)
            f = 0
            while f < F - HEAD:
                gather(f, emb1)
                f += 1
            for i in range(-HEAD, 0):
                gather(f, emb1)
                f += 1
                subtract(PAIR_KINDS, 0, i)

            def turn(kinds, j, gathers):
                f = 0
                first, lead = 22, 4
                step = (PAIR - 1 - first - lead) / F
                for i in range(len(kinds)):
                    subtract(kinds, j, i)
                    if gathers and i == first:
                        pool.wait_ge(gathered, 16 * F * (j + 2))
                        pool.wait_ge(transposed, 4 * (j + 2))
                        load_ids(j + 2)
                    if gathers and i == first + lead:
                        pool.wait_ge(idx_loaded, 16 * (j + 3))
                        pool.nop(nofuse=True)
                    while gathers and f < F and i >= first + lead + f * step:
                        gather(f, emb)
                        f += 1
                assert not gathers or f == F

            with pool.Fori(0, NB - 2) as j:
                turn(PAIR_KINDS, j, True)
            turn(PAIR_KINDS, NB - 2, False)
            turn(LAST_KINDS, NB - 1, False)

        @block.sync
        def _(sp):
            w0v = w0.rearrange("(f g) l -> f g l", f=F)
            sp.dma_start(w0_cols[:, 0:F, :], w0v).then_inc(w0_copied, 16)
            sp.dma_start(w0_cols[:, F:XR, :], w0v[:, 0:XR - F, :]).then_inc(w0_copied, 16)
            sp.dma_start(w0_rows[0:F, :, :], w0v).then_inc(w0_copied, 16)
            sp.dma_start(w0_rows[F:XR, :, :], w0v[0:XR - F, :, :]).then_inc(w0_copied, 16)
            full = P * (T1 - 1)
            for w, n, cols in ((w1, 1, ((0, H, H), (H, 0, H))), (w2, 2, ((0, 0, L),))):
                for to, fr, m in cols:
                    sp.dma_start(stage[n][:, 0:T1 - 1, to:to + m],
                                 w[0:full, fr:fr + m].rearrange("(t p) l -> p t l", p=P)).then_inc(weights_loaded, 16)
                    sp.dma_start(stage[n][0:H, T1 - 1, to:to + m],
                                 w[full:full + H, fr:fr + m]).then_inc(weights_loaded, 16)
            with nc.allow_non_contiguous_dma(reason="a few small columns"):
                sp.dma_start(bias0[:, :], b0.rearrange("(l o) -> l o", o=1)).then_inc(small_loaded, 16)
                b1v = b1.rearrange("(l o) -> l o", o=1)
                sp.dma_start(bias1[0:H, :], b1v[H:L, :]).then_inc(small_loaded, 16)
                sp.dma_start(bias1[H:L, :], b1v[0:H, :]).then_inc(small_loaded, 16)
                sp.dma_start(bias2[:, :], b2.rearrange("(l o) -> l o", o=1)).then_inc(small_loaded, 16)
                sp.dma_start(bt1[:, :], b_top1.rearrange("(m p) -> p m", p=P)).then_inc(small_loaded, 16)
                sp.dma_start(bt2[:, :], b_top2.rearrange("(m p) -> p m", p=P)).then_inc(small_loaded, 16)
                sp.dma_start(wt3[:, :], w_top3.rearrange("(m p) o -> p (m o)", p=P)).then_inc(small_loaded, 16)
            sp.wait_ge(w0_copied, 64)
            sp.wait_ge(w0_zeroed, 1)
            for t in range(T0):
                for k in range(K):
                    s = K * t + k
                    if s < SH:
                        cols = bass.AP(w0_cols.tensor, s * L, [[(XR + 1) * L, F], [1, L]])
                        sp.dma_start(stage[0][k:R0:K, t, :], cols).then_inc(w0_loaded, 16)
                    if 0 < s < SH:
                        rows = bass.AP(w0_rows.tensor, s * F * L, [[(F + 1) * L, F], [1, L]])
                        sp.dma_start(w0t[k:R0:K, t, :], rows).then_inc(w0_loaded, 16)

            def load_xk(b, half):
                for k in range(K):
                    src = bass.AP(xT.tensor, (2 * b + half) * XR * N, [[N, F], [1, N]])
                    sp.dma_start(xk[k:R0:K, :], src).then_inc(xk_loaded, 16)

            def load_xs(t, b, half):
                for k in range(K):
                    src = bass.AP(xT.tensor, ((2 * b + half) * XR + K * t + k) * N, [[N, F], [1, N]])
                    sp.dma_start(xs[k:R0:K, t % XS_RING, :], src).then_inc(xs_loaded[t % XS_RING], 16)

            def load_xr(q, b, half):
                for par in range(2):
                    n = 2 if 4 * q + 2 + par < F else 1
                    src = bass.AP(xT.tensor, ((2 * b + half) * XR + 4 * q + par) * N, [[0, H], [2 * N, n], [1, N]])
                    sp.dma_start(xr[par * H:par * H + H, 2 * q:2 * q + n, :], src).then_inc(xr_loaded[q], 16)

            def first_xs(b, half):
                load_xk(b, half)
                for t in range(XS_RING):
                    load_xs(t, b, half)

            def round_loads(s, j, i, b, half, b2, half2):
                for t in range(XS_RING, T0):
                    sp.wait_ge(z_ready, start(j) + i + t - XS_RING + 1)
                    load_xs(t, b, half)
                for q in range(T1 // 2):
                    sp.wait_ge(z_ready, start(j) + i + T0 + 2 * q + 2)
                    load_xr(q, b, half)
                if b2 is not None:
                    sp.wait_ge(xT_written[half2], 32 * (b2 + 1))
                    first_xs(b2, half2)

            sp.wait_ge(xT_written[0], 32)
            first_xs(0, 0)
            sp.wait_ge(w_lo, sum(len(k) - k.count("F") for k in KINDS.values()))
            sp.wait_ge(w_hi, sum(len(k) for k in KINDS.values()))
            for t in range(XS_RING, T0):
                sp.wait_ge(z_ready, t - XS_RING + 1)
                load_xs(t, 0, 0)
                load_xr(t - XS_RING, 0, 0)
            for q in range(T0 - XS_RING, T1 // 2):
                load_xr(q, 0, 0)
            sp.wait_ge(z_ready, T0)
            sp.wait_ge(xT_written[1], 32)
            first_xs(0, 1)
            with sp.Fori(0, NB - 1) as j:
                round_loads(2 * j, j, 0, j, 1, j + 1, 0)
                round_loads(2 * j + 1, j, ROUND, j + 1, 0, j + 1, 1)
            round_loads(NST - 2, NB - 1, 0, NB - 1, 1, None, None)
            sp.wait_ge(z_ready, start(NB - 1) + ROUND + 9)
            sp.dma_start(dn, dense.rearrange("(j p) c -> p j c", p=P)).then_inc(dense_loaded, 16)
            sp.wait_ge(z_ready, start(NB - 1) + ROUND + TOP_SLOTS)
            sp.dma_start(wA[0:H, :], w_top1[H:2 * H, :]).then_inc(top_loaded, 16)
            sp.dma_start(wA[H:P, :], w_top1[0:H, :]).then_inc(top_loaded, 16)
            sp.dma_start(wB[:, :], w_top1[P:2 * P, :]).then_inc(top_loaded, 16)
            sp.dma_start(wC[:, :], w_top1[2 * P:2 * P + DN, :]).then_inc(top_loaded, 16)
            sp.dma_start(wt2[:, :, :], w_top2.rearrange("(k p) n -> p k n", p=P)).then_inc(top_loaded, 16)
            sp.wait_ge(top_read, 14)
            sp.dma_start(out.rearrange("b o -> o b"), y).then_inc(out_written, 16)
            sp.wait_ge(out_written, 16)

        @block.vector
        def _(dve):
            nc.vector.memset(xr[:, 0:2, :], 0.0).then_inc(w0_zeroed, 1)

            def weight_lo(n, t, m):
                dve.wait_ge(w_hi, m + 1)
                dst, q = wl[n], split_at(n, t)
                nc.vector.tensor_tensor(dst[:, q, :], stage[n][:, t, :], wh[n][:, q, :], ALU.subtract).then_inc(w_lo, 1)

            dve.wait_ge(w0_loaded, 16 * (2 * SH - 1))
            nc.vector.tensor_tensor(stage[0], stage[0], w0t, ALU.add).then_inc(w0_summed, 1)
            m = 0
            for n in (1, 2, 0):
                for t in range(len(KINDS[n])):
                    if KINDS[n][t] != "F":
                        weight_lo(n, t, m)
                    m += 1

            def product(kinds, j, i, s):
                n, t = which_tile(kinds, i)
                m = before(i)
                if m >= -HEAD and kind(kinds, m) == "G":
                    dve.wait_ge(lo_pool, total("G", j) + splits(kinds, m, "G"))
                if m >= -HEAD and kind(kinds, m) == "D":
                    dve.wait_ge(lo_dve, total("D", j) + splits(kinds, m, "D"))
                if m >= -HEAD and kind(kinds, m) == "F":
                    dve.wait_ge(z_used, start(j) + m + 1)
                if n == 0:
                    if t == 0:
                        dve.wait_ge(xk_loaded, 16 * K * (s + 1))
                    r, loads = t % XS_RING, len(range(t % XS_RING, T0, XS_RING))
                    dve.wait_ge(xs_loaded[r], 16 * K * (loads * s + t // XS_RING + 1))
                    nc.vector.tensor_tensor(z[0:R0, slot(i), :], xk[:, :], xs[:, r, :], ALU.mult).then_inc(z_ready, 1)
                else:
                    if t == 0 and n == 1:
                        dve.wait_ge(read0, 3 * (s + 1))
                    if t == 0 and n == 2:
                        dve.wait_ge(read1, 3 * (s + 1))
                    if t % 2 == 0 and n == 1:
                        dve.wait_ge(xr_loaded[t // 2], 32 * (s + 1))
                    r, h = rows1(t), h1 if n == 1 else h2
                    nc.vector.tensor_tensor(z[0:r, slot(i), :], xr[0:r, t, :], h[0:r, :], ALU.mult).then_inc(z_ready, 1)

            def subtract(kinds, j, i):
                if i >= -HEAD and kind(kinds, i) == "D":
                    n, t = which_tile(kinds, i)
                    r = R0 if n == 0 else rows1(t)
                    q = split_slot(kinds, i)
                    dve.wait_ge(hi_ready, total("DG", j) + splits(kinds, i))
                    nc.vector.tensor_tensor(zl[0:r, q, :], z[0:r, slot(i), :], zh[0:r, q, :],
                                            ALU.subtract).then_inc(lo_dve, 1)

            def sum_d(src, s, half, b, which, total_):
                dst = total_[:, bass.ds(b * P, P)]
                if half and which == 1:
                    dve.wait_ge(add_done, 2 * b + 1)
                nc.vector.tensor_reduce(part[:] if half else dst, src[:].rearrange("p (d b) -> p b d", d=HD),
                                        AX.X, ALU.add).then_inc(sum_done, 1)
                if half:
                    dve.wait_ge(sum_done, 2 * s + 1 + which)
                    nc.vector.tensor_tensor(dst, dst, part[:], ALU.add).then_inc(add_done, 1)

            def round_(kinds, s, j, i0, b, half):
                for u in range(ROUND):
                    i = i0 + u
                    if u == T0:
                        dve.wait_ge(read1, 3 * (s + 1))
                        sum_d(direct, s, half, b, 0, zA)
                    if u == T0 + T1 + 8:
                        dve.wait_ge(read2, s + 1)
                        sum_d(last, s, half, b, 1, zB)
                    product(kinds, j, i, s if T0 <= u < T0 + T1 else s + 1)
                    subtract(kinds, j, i - LAG_SUB)

            for i in range(-HEAD, -T1):
                product(PAIR_KINDS, 0, i, 0)
                subtract(PAIR_KINDS, 0, i - LAG_SUB)
            for i in range(-T1 - LAG_SUB, -T1):
                subtract(PAIR_KINDS, 0, i)
            for i in range(-T1, 0):
                product(PAIR_KINDS, 0, i, 0)
                if i - LAG_SUB >= -T1:
                    subtract(PAIR_KINDS, 0, i - LAG_SUB)
            with dve.Fori(0, NB - 1) as j:
                round_(PAIR_KINDS, 2 * j, j, 0, j, 0)
                round_(PAIR_KINDS, 2 * j + 1, j, ROUND, j, 1)
            round_(LAST_KINDS, NST - 2, NB - 1, 0, NB - 1, 0)
            for i in range(ROUND - LAG_SUB, ROUND):
                subtract(LAST_KINDS, NB - 1, i)
            for i in range(ROUND, ROUND + T1 + LAG_SUB):
                if i < ROUND + T1:
                    product(LAST_KINDS, NB - 1, i, NST - 1)
                if i - LAG_SUB >= ROUND:
                    subtract(LAST_KINDS, NB - 1, i - LAG_SUB)
            dve.wait_ge(read1, 3 * NST)
            sum_d(direct, NST - 1, 1, NB - 1, 0, zA)
            dve.wait_ge(read2, NST)
            sum_d(last, NST - 1, 1, NB - 1, 1, zB)

        @block.scalar
        def _(act):
            def weight_hi(n, t):
                if KINDS[n][t] == "F":
                    dst = wf[n][:, full_at(n, t), :]
                else:
                    dst = wh[n][:, split_at(n, t), :]
                r = P if n == 0 else rows1(t)
                nc.scalar.activation(dst[0:r, :], stage[n][0:r, t, :], ACT.Copy).then_inc(w_hi, 1)

            act.wait_ge(weights_loaded, 16 * 6)
            for n in (1, 2, 0):
                if n == 0:
                    act.wait_ge(w0_summed, 1)
                for t in range(len(KINDS[n])):
                    weight_hi(n, t)

            def hi(kinds, j, i):
                if kind(kinds, i) != "F":
                    n, t = which_tile(kinds, i)
                    r = R0 if n == 0 else rows1(t)
                    act.wait_ge(z_ready, start(j) + i + 1)
                    m = split_before(kinds, i)
                    if m is not None:
                        act.wait_ge(z_used, start(j) + m + 1)
                    nc.scalar.activation(zh[0:r, split_slot(kinds, i), :], z[0:r, slot(i), :],
                                         ACT.Copy).then_inc(hi_ready, 1)

            def copy_xc(b, half, cur, first=False):
                if half == 1:
                    act.wait_ge(xT_written[0], 32 * (b + 1))
                elif not first:
                    act.wait_ge(xT_written[1], 32 * b)
                for r in range(2):
                    act.wait_ge(transposed, 4 * b + 2 * half + r + 1)
                    nc.scalar.activation(xc[:, r * BK:(r + 1) * BK], cur[0:F, r * BK:(r + 1) * BK],
                                         ACT.Copy).then_inc(xc_copied, 1)
                act.wait_ge(xc_copied, 4 * b + 2 * half + 2)
                to = xT[bass.ds(b, 1), half, :, :].rearrange("o f c -> (o f) c")
                act.dma_start(to[0:F, :], xc[:, :]).then_inc(xT_written[half], 16)
                act.dma_start(to[F:XR, :], xc[0:XR - F, :]).then_inc(xT_written[half], 16)

            def relu(dst, src, bias, done):
                nc.scalar.activation(dst, src, ACT.Relu, bias=bias).then_inc(done, 1)

            def take0(s, cur, first=False):
                relu(h1[0:H, :], cur[0:H, :], bias0[0:H, :], read0)
                relu(h1[H:P, :], cur[0:H, :], bias0[0:H, :], read0)
                if not first:
                    act.wait_ge(sum_done, 2 * s - 1)
                relu(direct[H:P, :], cur[H:P, :], bias0[H:P, :], read0)

            def take1(cur):
                relu(h2[0:H, :], cur[H:P, :], bias1[H:P, :], read1)
                relu(h2[H:P, :], cur[H:P, :], bias1[H:P, :], read1)
                relu(direct[0:H, :], cur[0:H, :], bias1[0:H, :], read1)

            def take2(cur, b=None):
                if b is not None:
                    act.wait_ge(xT_written[1], 32 * (b + 1))
                relu(last[:, :], cur[:, :], bias2[:, :], read2)

            copy_xc(0, 0, curA, first=True)
            copy_xc(0, 1, curB)
            act.wait_ge(small_loaded, 16 * 7)
            for i in range(-HEAD, 0):
                hi(PAIR_KINDS, 0, i)
                if i == -T1 - 1:
                    act.wait_ge(z_used, T0)
                    take0(0, curA, first=True)
            act.wait_ge(gathered, 2 * 16 * F)
            act.wait_ge(transposed, 4)
            nc.scalar.activation(emb[:, :], emb1, ACT.Copy).then_inc(emb_copied, 1)

            def round_(kinds, s, j, i0, cur, other, b_next):
                for u in range(ROUND):
                    i = i0 + u
                    hi(kinds, j, i)
                    if u == LAG_READ - 1:
                        act.wait_ge(z_used, start(j) + i0)
                        take1(other)
                    if u == T0 - 1 + LAG_READ:
                        act.wait_ge(z_used, start(j) + i0 + T0)
                        take0(s + 1, cur)
                    if b_next is not None and u in (T0 + 7, T0 + 13):
                        copy_xc(b_next, int(u == T0 + 13), cur)
                    if u == T0 + T1 - 1 + LAG_READ:
                        act.wait_ge(z_used, start(j) + i0 + T0 + T1)
                        take2(other, b_next)

            with act.Fori(0, NB - 1) as j:
                round_(PAIR_KINDS, 2 * j, j, 0, curA, curB, j + 1)
                round_(PAIR_KINDS, 2 * j + 1, j, ROUND, curB, curA, None)
            j = NB - 1
            round_(LAST_KINDS, NST - 2, j, 0, curA, curB, None)
            act.wait_ge(z_used, start(j) + ROUND)
            take1(curA)
            for i in range(ROUND, ROUND + T1):
                hi(LAST_KINDS, j, i)
                if i == ROUND + 18:
                    act.wait_ge(dense_turned, 1)
                    nc.scalar.activation(zC, h1[0:DN, :], ACT.Copy).then_inc(dense_copied, 1)
            act.wait_ge(z_used, start(j) + ROUND + T1)
            take2(curB)

            ps = (h1, curA, h2, curB)
            g = 0
            for n in range(NBK):
                for m in range(M1 // P):
                    act.wait_ge(top_done, g + 1)
                    relu(hid1[:, m, n * BK:(n + 1) * BK], ps[g // 2][:, (g % 2) * BK:(g % 2 + 1) * BK],
                         bt1[:, m:m + 1], top_read)
                    g += 1
            for n in range(NBK):
                for m in range(M2 // P):
                    act.wait_ge(top_done, g + 1)
                    relu(hid2[:, m, n * BK:(n + 1) * BK], ps[(g % 8) // 2][:, (g % 2) * BK:(g % 2 + 1) * BK],
                         bt2[:, m:m + 1], top_read)
                    g += 1
            for n in range(NBK):
                act.wait_ge(top_done, g + 1)
                nc.scalar.activation(y[:, n * BK:(n + 1) * BK], ps[(g % 8) // 2][0:1, (g % 2) * BK:(g % 2 + 1) * BK],
                                     ACT.Copy).then_inc(top_read, 1)
                g += 1

        @block.tensor
        def _(pe):
            def transposes(half, cur):
                ev = emb[:, :].rearrange("p (f d) -> p f d", d=D)
                for r in range(2):
                    for c in range(4):
                        mm = nc.tensor.transpose(cur[0:F, r * BK + c * P:r * BK + (c + 1) * P],
                                                 ev[:, :, HD * half + 4 * r + c], ident[:, :])
                    mm.then_inc(transposed, 1)

            def contract(kinds, j, i, cur, tiles):
                n, t = which_tile(kinds, i)
                r = R0 if n == 0 else rows1(t)
                first, stop = t == 0, t == tiles - 1

                def passes(w, v, start_, stop_):
                    for b in range(NBK):
                        mm = nc.tensor.matmul(cur[:, b * BK:(b + 1) * BK], w[0:r, :], v[0:r, b * BK:(b + 1) * BK],
                                              start=start_, stop=stop_)
                    return mm

                if kind(kinds, i) == "F":
                    pe.wait_ge(z_ready, start(j) + i + 1)
                    mm = passes(wf[n][:, full_at(n, t), :], z[:, slot(i), :], first, stop)
                else:
                    q, w = split_slot(kinds, i), split_at(n, t)
                    pe.wait_ge(hi_ready, total("DG", j) + splits(kinds, i))
                    passes(wl[n][:, w, :], zh[:, q, :], first, False)
                    passes(wh[n][:, w, :], zh[:, q, :], False, False)
                    lo = lo_dve if kind(kinds, i) == "D" else lo_pool
                    pe.wait_ge(lo, total(kind(kinds, i), j) + splits(kinds, i, kind(kinds, i)))
                    mm = passes(wh[n][:, w, :], zl[:, q, :], False, stop)
                mm.then_inc(z_used, 1)

            pe.wait_ge(ident_ready, 1)
            pe.wait_ge(gathered, 16 * F)
            transposes(0, curA)
            transposes(1, curB)
            pe.wait_ge(w_hi, sum(len(k) for k in KINDS.values()))
            pe.wait_ge(w_lo, sum(len(k) - k.count("F") for k in KINDS.values()))
            pe.wait_ge(xc_copied, 4)
            for i in range(-HEAD, 0):
                if i < -T1:
                    contract(PAIR_KINDS, 0, i, curA, T0)
                else:
                    contract(PAIR_KINDS, 0, i, curB, T1)

            def round_(kinds, s, j, i0, cur, other, b_next):
                for u in range(T0):
                    contract(kinds, j, i0 + u, cur, T0)
                pe.wait_ge(read1, 3 * (s + 1))
                for u in range(T0, T0 + T1):
                    contract(kinds, j, i0 + u, other, T1)
                    if b_next is not None and u == T0 + 4:
                        pe.wait_ge(read0, 3 * (s + 2))
                        pe.wait_ge(emb_copied, 1)
                        pe.wait_ge(gathered, 16 * F * (b_next + 1))
                        pe.nop(nofuse=True)
                        transposes(0, cur)
                    if b_next is not None and u == T0 + 10:
                        pe.wait_ge(xc_copied, 4 * b_next + 2)
                        pe.nop(nofuse=True)
                        transposes(1, cur)
                pe.wait_ge(read0, 3 * (s + 2))
                if b_next is not None:
                    pe.wait_ge(xc_copied, 4 * b_next + 4)
                for u in range(T0 + T1, ROUND):
                    contract(kinds, j, i0 + u, cur, T1)

            with pe.Fori(0, NB - 1) as j:
                round_(PAIR_KINDS, 2 * j, j, 0, curA, curB, j + 1)
                round_(PAIR_KINDS, 2 * j + 1, j, ROUND, curB, curA, None)
            j = NB - 1
            round_(LAST_KINDS, NST - 2, j, 0, curA, curB, None)
            pe.wait_ge(read2, NST - 1)
            for i in range(ROUND, ROUND + T1):
                contract(LAST_KINDS, j, i, curB, T1)
                if i == ROUND + 16:
                    pe.wait_ge(dense_loaded, 16)
                    for c in range(NB):
                        mm = nc.tensor.transpose(h1[0:DN, c * P:(c + 1) * P], dn[:, c, :], ident[:, :])
                    mm.then_inc(dense_turned, 1)

            ps = (h1, curA, h2, curB)

            def bank(g):
                return ps[(g % 8) // 2][:, (g % 2) * BK:(g % 2 + 1) * BK]

            pe.wait_ge(top_loaded, 16 * 5)
            pe.wait_ge(dense_copied, 1)
            pe.wait_ge(read1, 3 * NST)
            pe.wait_ge(add_done, 2 * NB - 2)
            g = 0
            for n in range(NBK):
                if n == 1:
                    pe.wait_ge(read2, NST)
                    pe.wait_ge(add_done, 2 * NB)
                for m in range(M1 // P):
                    parts = ((wA, zA), (wB, zB), (wC, zC))
                    for q, (w, v) in enumerate(parts):
                        mm = nc.tensor.matmul(bank(g), w[:, m * P:(m + 1) * P], v[:, n * BK:(n + 1) * BK],
                                              start=(q == 0), stop=(q == len(parts) - 1))
                    mm.then_inc(top_done, 1)
                    g += 1
            for n in range(NBK):
                pe.wait_ge(top_read, (n + 1) * (M1 // P))
                for m in range(M2 // P):
                    if g - 8 >= (n + 1) * (M1 // P):
                        pe.wait_ge(top_read, g - 7)
                    for q in range(M1 // P):
                        mm = nc.tensor.matmul(bank(g), wt2[:, q, m * P:(m + 1) * P], hid1[:, q, n * BK:(n + 1) * BK],
                                              start=(q == 0), stop=(q == M1 // P - 1))
                    mm.then_inc(top_done, 1)
                    g += 1
            for n in range(NBK):
                pe.wait_ge(top_read, NBK * M1 // P + (n + 1) * (M2 // P))
                for q in range(M2 // P):
                    mm = nc.tensor.matmul(bank(g)[0:1, :], wt3[:, q:q + 1], hid2[:, q, n * BK:(n + 1) * BK],
                                          start=(q == 0), stop=(q == M2 // P - 1))
                mm.then_inc(top_done, 1)
                g += 1


_TBL = [f"tbl_{f}" for f in range(F)]
_INS = (["dense_ctx", "ids"] + _TBL + ["W_top1", "b_top1", "W_top2", "b_top2", "W_top3"]
        + ["L0_rec_W0", "L0_rec_W1", "L0_rec_W2", "L0_rec_b0", "L0_rec_b1", "L0_rec_b2"])


def kernel(**inputs):
    import numpy as _np
    import concourse.bacc as _bacc
    from concourse import mybir as _mybir
    from concourse.bass_utils import run_bass_kernel_spmd as _run

    nc = _bacc.Bacc("TRN2", target_bir_lowering=False, num_devices=1)
    arrays, aps = {}, {}
    for name in _INS:
        a = _np.ascontiguousarray(inputs[name])
        arrays[f"in_{name}_dram"] = a
        aps[name] = nc.dram_tensor(f"in_{name}_dram", a.shape, _mybir.dt.from_np(a.dtype), kind="ExternalInput").ap()
    out = nc.dram_tensor("out_0_dram", (B, 1), F32, kind="ExternalOutput").ap()
    args = [aps["dense_ctx"], aps["ids"], [aps[n] for n in _TBL]] + [aps[n] for n in _INS[2 + F:]]
    cin_tower(nc, *args, out)
    r = _run(nc, [arrays], core_ids=[0])
    return r.results[0]["out_0_dram"]
```

```python
from contextlib import ExitStack

import concourse.bass as bass
from concourse import mybir

F32 = mybir.dt.float32
I32 = mybir.dt.int32
U32 = mybir.dt.uint32
ALU = mybir.AluOpType
ACT = mybir.ActivationFunctionType
AX = mybir.AxisListType

P = 128
B, F, D, L = 1024, 39, 16, 128
H = L // 2
NB = B // P
HD = D // 2
N = HD * P
BK = 512
NBK = N // BK
NST = 2 * NB
K = 3
SH = (F + 1) // 2
T0 = -(-SH // K)
R0 = K * F
XR = F + T0 * K - 1
T1 = -(-F // 2)
DN = 16
M1, M2 = 512, 256
F32R = mybir.dt.float32r

KINDS0 = "FDFGFDF"
KINDS1 = "FGDFGFGDFGFGDFGFGDGF"
KINDS = {0: KINDS0, 1: KINDS1, 2: KINDS1}

ROUND = T0 + 2 * T1
PAIR = 2 * ROUND
HEAD = T0 + T1
ROUND_KINDS = KINDS[0] + KINDS[2] + KINDS[1]
HEAD_KINDS = KINDS[0] + KINDS[1]
PAIR_KINDS = ROUND_KINDS + ROUND_KINDS
LAST_KINDS = ROUND_KINDS + KINDS[2]
RING = 6
HI_RING = 5
LO_RING = 3
XS_RING = 5
LAG_SUB = 2
LAG_READ = 5
LAG_DIRECT = 0


def kind(kinds, i):
    return kinds[i] if i >= 0 else HEAD_KINDS[i + HEAD]


def splits(kinds, i, which="DG"):
    if i >= 0:
        return sum(k in which for k in kinds[:i + 1])
    return -sum(k in which for k in HEAD_KINDS[i + 1 + HEAD:])


def total(which, j):
    return sum(k in which for k in HEAD_KINDS) + j * sum(k in which for k in PAIR_KINDS)


def slot(i):
    return i % RING if i >= 0 else (PAIR + i) % RING


def split_slot(kinds, i, ring):
    n = splits(kinds, i) - 1
    return n % ring if n >= 0 else (splits(PAIR_KINDS, PAIR - 1) + n) % ring


def before(i):
    m = i - 1
    while slot(m) != slot(i):
        m -= 1
    return m


def split_before(kinds, i, ring):
    m = i - 1
    while m >= -HEAD and (kind(kinds, m) == "F" or split_slot(kinds, m, ring) != split_slot(kinds, i, ring)):
        m -= 1
    return m if m >= -HEAD else None


def start(j):
    return HEAD + PAIR * j


def rows1(t):
    return P if 2 * t + 1 < F else H


def which_tile(kinds, i):
    if i < 0:
        i += HEAD
        return (0, i) if i < T0 else (1, i - T0)
    if kinds is LAST_KINDS and i >= ROUND:
        return 2, i - ROUND
    i %= ROUND
    return (0, i) if i < T0 else (2, i - T0) if i < T0 + T1 else (1, i - T0 - T1)


def cin_tower(nc, dense, ids, tables, w_top1, b_top1, w_top2, b_top2, w_top3, w0, w1, w2, b0, b1, b2, out):
    xT = nc.dram_tensor("xT", [NB, 2, XR, N], F32, kind="Internal").ap()
    zT = nc.dram_tensor("zT", [2, P, B], F32, kind="Internal").ap()
    w0_cols = nc.dram_tensor("w0_cols", [F, XR, L], F32, kind="Internal").ap()
    w0_rows = nc.dram_tensor("w0_rows", [XR, F, L], F32, kind="Internal").ap()

    with ExitStack() as ctx:
        def sb(name, shape, dt=F32):
            return ctx.enter_context(nc.sbuf_tensor(name, shape, dt))

        def sem(name):
            return ctx.enter_context(nc.semaphore(name))

        curA, curB, h1, h2 = [ctx.enter_context(nc.psum_tensor(n, [P, N], F32)) for n in ("curA", "curB", "h1", "h2")]

        ident = sb("ident", [P, P])
        idx = sb("idx", [P, F], I32)
        emb = sb("emb", [P, F * D])
        xk = sb("xk", [P, N])
        xs = sb("xs", [P, XS_RING, N])
        xr = sb("xr", [P, T1 - 1, N])
        xl = sb("xl", [P, BK])
        z = sb("z", [P, RING, N])
        zh = sb("zh", [P, HI_RING, N], F32R)
        zl = sb("zl", [P, LO_RING, N], F32R)
        direct = sb("direct", [P, N])
        xc = direct[0:F, :]
        zs = sb("zs", [P, 2, P])
        part = sb("part", [P, P])
        bias0 = sb("bias0", [P, 1])
        bias1 = sb("bias1", [P, 1])
        bias2 = sb("bias2", [P, 1])
        bt1 = sb("bt1", [P, M1 // P])
        bt2 = sb("bt2", [P, M2 // P])
        wt3 = sb("wt3", [P, M2 // P])
        wf = {n: sb(f"wf{n}", [P, KINDS[n].count("F"), L]) for n in KINDS}
        wh = {n: sb(f"wh{n}", [P, len(KINDS[n]) - KINDS[n].count("F"), L], F32R) for n in KINDS}
        wl = {n: sb(f"wl{n}", [P, len(KINDS[n]) - KINDS[n].count("F"), L], F32R) for n in KINDS}

        def full_at(n, t):
            return KINDS[n][:t].count("F")

        def split_at(n, t):
            return t - full_at(n, t)

        per = N // L
        stage = {0: xr[:, 0:1, :].rearrange("p a (t l) -> p (a t) l", l=L)[:, 0:T0, :],
                 1: xr[:, 2:2 + -(-T1 // per), :].rearrange("p a (t l) -> p (a t) l", l=L)[:, 0:T1, :],
                 2: xr[:, 5:5 + -(-T1 // per), :].rearrange("p a (t l) -> p (a t) l", l=L)[:, 0:T1, :]}
        w0t = xr[:, 1:2, :].rearrange("p a (t l) -> p (a t) l", l=L)[:, 0:T0, :]

        n0, n1 = slice(0, BK), slice(BK, N)
        wA, wB, wC = xs[:, 0, n0], xs[:, 0, n1], xs[0:DN, 1, n0]
        dn = xs[:, 1, M1:M1 + NB * DN].rearrange("p (j c) -> p j c", c=DN)
        zC = xs[0:DN, 2, :]
        zAB = (xs[:, 3, :].rearrange("p (w c) -> p w c", w=2), xr[:, 7, :].rearrange("p (w c) -> p w c", w=2))
        hid1 = ((xk[:, n0], xk[:, n1], xr[:, 0, n0], xr[:, 0, n1]),
                (xr[:, 1, n0], xr[:, 1, n1], xr[:, 2, n0], xr[:, 2, n1]))
        hid2 = ((xr[:, 3, n0], xr[:, 3, n1]), (xr[:, 4, n0], xr[:, 4, n1]))
        y = xr[0:1, 5, :]
        wt2 = xr[:, 6, :].rearrange("p (k n) -> p k n", n=M2)
        EARLY = 4
        GROUPS = [(1, 0, 0, curB, n0), (1, 0, 1, curB, n1), (1, 0, 2, h1, n0), (1, 0, 3, h1, n1),
                  (2, 0, 0, h1, n0), (2, 0, 1, h1, n1),
                  (1, 1, 0, curB, n0), (1, 1, 1, curB, n1), (1, 1, 2, h2, n0), (1, 1, 3, h2, n1),
                  (2, 1, 0, curA, n0), (2, 1, 1, curA, n1), (3, 0, 0, h1, n0), (3, 1, 0, h1, n1)]

        def groups_before(layer, half):
            return 1 + max(g for g, (l, n, *_) in enumerate(GROUPS) if (l, n) == (layer, half))

        ident_zeroed = sem("ident_zeroed")
        ident_ready = sem("ident_ready")
        idx_loaded = sem("idx_loaded")
        gathered = sem("gathered")
        small_loaded = sem("small_loaded")
        weights_loaded = sem("weights_loaded")
        w0_copied = sem("w0_copied")
        w0_zeroed = sem("w0_zeroed")
        w0_loaded = sem("w0_loaded")
        w0_summed = sem("w0_summed")
        w_hi = sem("w_hi")
        w_lo = sem("w_lo")
        transposed = sem("transposed")
        xc_copied = sem("xc_copied")
        xT_written = [sem(f"xT_written{h}") for h in range(2)]
        xk_loaded = sem("xk_loaded")
        xs_loaded = [sem(f"xs_loaded{r}") for r in range(XS_RING)]
        xr_loaded = [sem(f"xr_loaded{q}") for q in range(T1 // 2)]
        z_ready = sem("z_ready")
        hi_ready = sem("hi_ready")
        lo_dve = sem("lo_dve")
        lo_pool = sem("lo_pool")
        z_used = sem("z_used")
        read0 = sem("read0")
        read1 = sem("read1")
        read2 = sem("read2")
        z_stored = [sem(f"z_stored{w}") for w in range(2)]
        sum_done = sem("sum_done")
        add_done = sem("add_done")
        top_loaded = sem("top_loaded")
        top2_loaded = sem("top2_loaded")
        dense_loaded = sem("dense_loaded")
        dense_turned = sem("dense_turned")
        dense_copied = sem("dense_copied")
        top_done = sem("top_done")
        top_read = sem("top_read")
        out_written = sem("out_written")

        block = ctx.enter_context(nc.Block())

        @block.gpsimd
        def _(pool):
            def load_ids(b):
                pool.dma_start(idx[:, :], ids[bass.ds(b * P, P), :]).then_inc(idx_loaded, 16)

            def gather(f):
                nc.gpsimd.indirect_dma_start(
                    out=emb[:, f * D:(f + 1) * D], out_offset=None, in_=tables[f],
                    in_offset=bass.IndirectOffsetOnAxis(ap=idx[:, f:f + 1].bitcast(U32), axis=0),
                ).then_inc(gathered, 16)

            def subtract(kinds, j, i):
                if kind(kinds, i) == "G":
                    n, t = which_tile(kinds, i)
                    r = R0 if n == 0 else rows1(t)
                    h, q = split_slot(kinds, i, HI_RING), split_slot(kinds, i, LO_RING)
                    m = split_before(kinds, i, LO_RING)
                    if m is not None:
                        pool.wait_ge(z_used, start(j) + m + 1)
                    pool.wait_ge(hi_ready, total("DG", j) + splits(kinds, i))
                    nc.gpsimd.tensor_tensor(zl[0:r, q, :], z[0:r, slot(i), :], zh[0:r, h, :],
                                            ALU.subtract).then_inc(lo_pool, 1)

            load_ids(0)
            nc.gpsimd.memset(ident[:], 1.0).then_inc(ident_zeroed, 1)
            pool.wait_ge(idx_loaded, 16)
            for f in range(F):
                gather(f)
            pool.wait_ge(ident_zeroed, 1)
            nc.gpsimd.affine_select(out=ident[:], in_=ident[:], compare_op=ALU.is_equal, fill=0.0, base=0,
                                    pattern=[[-1, P]], channel_multiplier=1).then_inc(ident_ready, 1)
            pool.wait_ge(gathered, 16 * F)
            load_ids(1)
            pool.wait_ge(idx_loaded, 32)
            pool.wait_ge(transposed, 4)
            f = 0
            while f < F - HEAD:
                gather(f)
                f += 1
            for i in range(-HEAD, 0):
                gather(f)
                f += 1
                subtract(PAIR_KINDS, 0, i)

            def turn(kinds, j, gathers):
                f = 0
                first, lead = 22, 4
                step = (PAIR - 1 - first - lead) / F
                for i in range(len(kinds)):
                    subtract(kinds, j, i)
                    if gathers and i == first:
                        pool.wait_ge(gathered, 16 * F * (j + 2))
                        pool.wait_ge(transposed, 4 * (j + 2))
                        load_ids(j + 2)
                    if gathers and i == first + lead:
                        pool.wait_ge(idx_loaded, 16 * (j + 3))
                        pool.nop(nofuse=True)
                    while gathers and f < F and i >= first + lead + f * step:
                        gather(f)
                        f += 1
                assert not gathers or f == F

            with pool.Fori(0, NB - 2) as j:
                turn(PAIR_KINDS, j, True)
            turn(PAIR_KINDS, NB - 2, False)
            turn(LAST_KINDS, NB - 1, False)

        @block.sync
        def _(sp):
            w0v = w0.rearrange("(f g) l -> f g l", f=F)
            sp.dma_start(w0_cols[:, 0:F, :], w0v).then_inc(w0_copied, 16)
            sp.dma_start(w0_cols[:, F:XR, :], w0v[:, 0:XR - F, :]).then_inc(w0_copied, 16)
            sp.dma_start(w0_rows[0:F, :, :], w0v).then_inc(w0_copied, 16)
            sp.dma_start(w0_rows[F:XR, :, :], w0v[0:XR - F, :, :]).then_inc(w0_copied, 16)
            full = P * (T1 - 1)
            for w, n, cols in ((w1, 1, ((0, H, H), (H, 0, H))), (w2, 2, ((0, 0, L),))):
                for to, fr, m in cols:
                    sp.dma_start(stage[n][:, 0:T1 - 1, to:to + m],
                                 w[0:full, fr:fr + m].rearrange("(t p) l -> p t l", p=P)).then_inc(weights_loaded, 16)
                    for p in (0, H):
                        sp.dma_start(stage[n][p:p + H, T1 - 1, to:to + m],
                                     w[full:full + H, fr:fr + m]).then_inc(weights_loaded, 16)
            with nc.allow_non_contiguous_dma(reason="a few small columns"):
                sp.dma_start(bias0[:, :], b0.rearrange("(l o) -> l o", o=1)).then_inc(small_loaded, 16)
                b1v = b1.rearrange("(l o) -> l o", o=1)
                sp.dma_start(bias1[0:H, :], b1v[H:L, :]).then_inc(small_loaded, 16)
                sp.dma_start(bias1[H:L, :], b1v[0:H, :]).then_inc(small_loaded, 16)
                sp.dma_start(bias2[:, :], b2.rearrange("(l o) -> l o", o=1)).then_inc(small_loaded, 16)
                sp.dma_start(bt1[:, :], b_top1.rearrange("(m p) -> p m", p=P)).then_inc(small_loaded, 16)
                sp.dma_start(bt2[:, :], b_top2.rearrange("(m p) -> p m", p=P)).then_inc(small_loaded, 16)
                sp.dma_start(wt3[:, :], w_top3.rearrange("(m p) o -> p (m o)", p=P)).then_inc(small_loaded, 16)
            sp.wait_ge(w0_copied, 64)
            sp.wait_ge(w0_zeroed, 1)
            for t in range(T0):
                for k in range(K):
                    s = K * t + k
                    if s < SH:
                        cols = bass.AP(w0_cols.tensor, s * L, [[(XR + 1) * L, F], [1, L]])
                        sp.dma_start(stage[0][k:R0:K, t, :], cols).then_inc(w0_loaded, 16)
                    if 0 < s < SH:
                        rows = bass.AP(w0_rows.tensor, s * F * L, [[(F + 1) * L, F], [1, L]])
                        sp.dma_start(w0t[k:R0:K, t, :], rows).then_inc(w0_loaded, 16)

            def load_xk(b, half):
                src = bass.AP(xT.tensor, (2 * b + half) * XR * N, [[N, F], [0, K], [1, N]])
                sp.dma_start(xk[0:R0, :], src).then_inc(xk_loaded, 16)

            def load_xs(t, b, half):
                src = bass.AP(xT.tensor, ((2 * b + half) * XR + K * t) * N, [[N, F], [N, K], [1, N]])
                sp.dma_start(xs[0:R0, t % XS_RING, :], src).then_inc(xs_loaded[t % XS_RING], 16)

            def load_xr(q, b, half):
                for par in range(2):
                    n = 1 if q == T1 // 2 - 1 else 2
                    src = bass.AP(xT.tensor, ((2 * b + half) * XR + 4 * q + par) * N, [[0, H], [2 * N, n], [1, N]])
                    sp.dma_start(xr[par * H:par * H + H, 2 * q:2 * q + n, :], src).then_inc(xr_loaded[q], 16)
                    if q == T1 // 2 - 1:
                        src = bass.AP(xT.tensor, ((2 * b + half) * XR + F - 1) * N + par * BK, [[0, H], [1, BK]])
                        sp.dma_start(xl[par * H:par * H + H, :], src).then_inc(xr_loaded[q], 16)

            def first_xs(b, half):
                load_xk(b, half)
                for t in range(XS_RING):
                    load_xs(t, b, half)

            def round_loads(s, j, i, b, half, b2, half2):
                for t in range(XS_RING, T0):
                    sp.wait_ge(z_ready, start(j) + i + t - XS_RING + 1)
                    load_xs(t, b, half)
                for q in range(T1 // 2):
                    sp.wait_ge(z_ready, start(j) + i + T0 + 2 * q + 2)
                    load_xr(q, b, half)
                if b2 is not None:
                    sp.wait_ge(xT_written[half2], 32 * (b2 + 1))
                    first_xs(b2, half2)

            sp.wait_ge(xT_written[0], 32)
            first_xs(0, 0)
            for t in range(XS_RING, T0):
                sp.wait_ge(z_ready, t - XS_RING + 1)
                load_xs(t, 0, 0)
            sp.wait_ge(w_lo, sum(len(k) - k.count("F") for k in KINDS.values()))
            sp.wait_ge(w_hi, sum(len(k) for k in KINDS.values()))
            for q in range(T1 // 2):
                load_xr(q, 0, 0)
            sp.wait_ge(z_ready, T0)
            sp.wait_ge(xT_written[1], 32)
            first_xs(0, 1)
            def store_z(b):
                for w in range(2):
                    sp.wait_ge(add_done, 2 * b + w + 1)
                    sp.dma_start(zT[w, :, bass.ds(b * P, P)], zs[:, w, :]).then_inc(z_stored[w], 16)

            with sp.Fori(0, NB - 1) as j:
                round_loads(2 * j, j, 0, j, 1, j + 1, 0)
                round_loads(2 * j + 1, j, ROUND, j + 1, 0, j + 1, 1)
                store_z(j)
            for t in range(XS_RING, T0):
                sp.wait_ge(z_ready, start(NB - 1) + t - XS_RING + 1)
                load_xs(t, NB - 1, 1)
            sp.wait_ge(z_ready, start(NB - 1) + T0)
            sp.dma_start(dn, dense.rearrange("(j p) c -> p j c", p=P)).then_inc(dense_loaded, 16)
            sp.dma_start(xs[0:H, 0, n0], w_top1[H:2 * H, :]).then_inc(top_loaded, 16)
            sp.dma_start(xs[H:P, 0, n0], w_top1[0:H, :]).then_inc(top_loaded, 16)
            sp.dma_start(wB, w_top1[P:2 * P, :]).then_inc(top_loaded, 16)
            sp.dma_start(wC, w_top1[2 * P:2 * P + DN, :]).then_inc(top_loaded, 16)
            for w in range(2):
                sp.wait_ge(z_stored[w], 16 * (NB - 1))
                sp.dma_start(zAB[0][:, w, :], zT[w, :, n0]).then_inc(top_loaded, 16)
            for q in range(T1 // 2):
                sp.wait_ge(z_ready, start(NB - 1) + T0 + 2 * q + 2)
                load_xr(q, NB - 1, 1)
            sp.wait_ge(z_ready, start(NB - 1) + ROUND + 8)
            sp.dma_start(wt2, w_top2.rearrange("(k p) n -> p k n", p=P)).then_inc(top2_loaded, 16)
            for w in range(2):
                sp.dma_start(zAB[1][:, w, 0:BK - P], zT[w, :, BK:B - P]).then_inc(top2_loaded, 16)
            sp.wait_ge(top_read, 14)
            sp.dma_start(out.rearrange("b o -> o b"), y).then_inc(out_written, 16)
            sp.wait_ge(out_written, 16)

        @block.vector
        def _(dve):
            nc.vector.memset(xr[:, 0:2, :], 0.0).then_inc(w0_zeroed, 1)

            def weight_lo(n, t, m):
                dve.wait_ge(w_hi, m + 1)
                dst, q = wl[n], split_at(n, t)
                nc.vector.tensor_tensor(dst[:, q, :], stage[n][:, t, :], wh[n][:, q, :], ALU.subtract).then_inc(w_lo, 1)

            dve.wait_ge(w0_loaded, 16 * (2 * SH - 1))
            nc.vector.tensor_tensor(stage[0], stage[0], w0t, ALU.add).then_inc(w0_summed, 1)
            m = 0
            for n in (1, 2, 0):
                for t in range(len(KINDS[n])):
                    if KINDS[n][t] != "F":
                        weight_lo(n, t, m)
                    m += 1

            def product(kinds, j, i, s):
                n, t = which_tile(kinds, i)
                m = before(i)
                if m >= -HEAD and kind(kinds, m) == "G":
                    dve.wait_ge(lo_pool, total("G", j) + splits(kinds, m, "G"))
                if m >= -HEAD and kind(kinds, m) == "D":
                    dve.wait_ge(lo_dve, total("D", j) + splits(kinds, m, "D"))
                if m >= -HEAD and kind(kinds, m) == "F":
                    dve.wait_ge(z_used, start(j) + m + 1)
                if n == 0:
                    if t == 0:
                        dve.wait_ge(xk_loaded, 16 * (s + 1))
                    r, loads = t % XS_RING, len(range(t % XS_RING, T0, XS_RING))
                    dve.wait_ge(xs_loaded[r], 16 * (loads * s + t // XS_RING + 1))
                    nc.vector.tensor_tensor(z[0:R0, slot(i), :], xk[0:R0, :], xs[0:R0, r, :], ALU.mult).then_inc(z_ready, 1)
                else:
                    if t == 0 and n == 1:
                        dve.wait_ge(read0, 3 * (s + 1))
                    if t == 0 and n == 2:
                        dve.wait_ge(read1, 3 * (s + 1))
                    if t % 2 == 0 and n == 1:
                        dve.wait_ge(xr_loaded[t // 2], (32 if t < T1 - 2 else 64) * (s + 1))
                    h = h1 if n == 1 else h2
                    if t < T1 - 1:
                        ins = nc.vector.tensor_tensor(z[:, slot(i), :], xr[:, t, :], h[:, :], ALU.mult)
                    else:
                        for b in range(NBK):
                            p = slice(b * H, b * H + H)
                            ins = nc.vector.tensor_tensor(z[p, slot(i), 0:BK], xl[p, :],
                                                          h[p, b * BK:(b + 1) * BK], ALU.mult)
                    ins.then_inc(z_ready, 1)

            def subtract(kinds, j, i):
                if i >= -HEAD and kind(kinds, i) == "D":
                    n, t = which_tile(kinds, i)
                    r = R0 if n == 0 else rows1(t)
                    h, q = split_slot(kinds, i, HI_RING), split_slot(kinds, i, LO_RING)
                    m = split_before(kinds, i, LO_RING)
                    if m is not None:
                        dve.wait_ge(z_used, start(j) + m + 1)
                    dve.wait_ge(hi_ready, total("DG", j) + splits(kinds, i))
                    nc.vector.tensor_tensor(zl[0:r, q, :], z[0:r, slot(i), :], zh[0:r, h, :],
                                            ALU.subtract).then_inc(lo_dve, 1)

            def sum_d(src, s, half, b, which, first=False, dst=None):
                if half == 0 and not first:
                    dve.wait_ge(z_stored[which], 16 * b)
                if half == 1 and which == 1:
                    dve.wait_ge(add_done, 2 * b + 1)
                nc.vector.tensor_reduce(part[:] if half else zs[:, which, :], src[:].rearrange("p (d b) -> p b d", d=HD),
                                        AX.X, ALU.add).then_inc(sum_done, 1)
                if half:
                    dve.wait_ge(sum_done, 2 * s + 1 + which)
                    nc.vector.tensor_tensor(zs[:, which, :] if dst is None else dst, zs[:, which, :], part[:],
                                            ALU.add).then_inc(add_done, 1)

            def round_(kinds, s, j, i0, b, half, first=False):
                for u in range(ROUND):
                    i = i0 + u
                    if u == T0 + 5:
                        dve.wait_ge(read1, 3 * (s + 1))
                        sum_d(direct, s, half, b, 0, first)
                    if u == T0 + T1 + 8:
                        dve.wait_ge(read2, s + 1)
                        sum_d(curA if half else curB, s, half, b, 1, first)
                    product(kinds, j, i, s if T0 <= u < T0 + T1 else s + 1)
                    subtract(kinds, j, i - LAG_SUB)

            for i in range(-HEAD, -T1):
                product(PAIR_KINDS, 0, i, 0)
                subtract(PAIR_KINDS, 0, i - LAG_SUB)
            for i in range(-T1 - LAG_SUB, -T1):
                subtract(PAIR_KINDS, 0, i)
            for i in range(-T1, 0):
                product(PAIR_KINDS, 0, i, 0)
                if i - LAG_SUB >= -T1:
                    subtract(PAIR_KINDS, 0, i - LAG_SUB)
            round_(PAIR_KINDS, 0, 0, 0, 0, 0, first=True)
            round_(PAIR_KINDS, 1, 0, ROUND, 0, 1)
            with dve.Fori(1, NB - 1) as j:
                round_(PAIR_KINDS, 2 * j, j, 0, j, 0)
                round_(PAIR_KINDS, 2 * j + 1, j, ROUND, j, 1)
            round_(LAST_KINDS, NST - 2, NB - 1, 0, NB - 1, 0)
            for i in range(ROUND - LAG_SUB, ROUND):
                subtract(LAST_KINDS, NB - 1, i)
            for i in range(ROUND, ROUND + T1 + LAG_SUB):
                if i < ROUND + T1:
                    product(LAST_KINDS, NB - 1, i, NST - 1)
                if i - LAG_SUB >= ROUND:
                    subtract(LAST_KINDS, NB - 1, i - LAG_SUB)
            dve.wait_ge(read1, 3 * NST)
            sum_d(direct, NST - 1, 1, NB - 1, 0, dst=zAB[1][:, 0, BK - P:BK])
            dve.wait_ge(read2, NST)
            sum_d(curA, NST - 1, 1, NB - 1, 1, dst=zAB[1][:, 1, BK - P:BK])

        @block.scalar
        def _(act):
            def weight_hi(n, t):
                if KINDS[n][t] == "F":
                    dst = wf[n][:, full_at(n, t), :]
                else:
                    dst = wh[n][:, split_at(n, t), :]
                nc.scalar.activation(dst, stage[n][:, t, :], ACT.Copy).then_inc(w_hi, 1)

            act.wait_ge(weights_loaded, 16 * 9)
            for n in (1, 2, 0):
                if n == 0:
                    act.wait_ge(w0_summed, 1)
                for t in range(len(KINDS[n])):
                    weight_hi(n, t)

            def hi(kinds, j, i):
                if kind(kinds, i) != "F":
                    n, t = which_tile(kinds, i)
                    r = R0 if n == 0 else rows1(t)
                    act.wait_ge(z_ready, start(j) + i + 1)
                    m = split_before(kinds, i, HI_RING)
                    if m is not None:
                        act.wait_ge(z_used, start(j) + m + 1)
                    nc.scalar.activation(zh[0:r, split_slot(kinds, i, HI_RING), :], z[0:r, slot(i), :],
                                         ACT.Copy).then_inc(hi_ready, 1)

            def copy_xc(b, half, cur, first=False):
                if half == 1:
                    act.wait_ge(xT_written[0], 32 * (b + 1))
                elif not first:
                    act.wait_ge(xT_written[1], 32 * b)
                for r in range(2):
                    act.wait_ge(transposed, 4 * b + 2 * half + r + 1)
                    nc.scalar.activation(xc[:, r * BK:(r + 1) * BK], cur[0:F, r * BK:(r + 1) * BK],
                                         ACT.Copy).then_inc(xc_copied, 1)
                act.wait_ge(xc_copied, 4 * b + 2 * half + 2)
                to = xT[bass.ds(b, 1), half, :, :].rearrange("o f c -> (o f) c")
                act.dma_start(to[0:F, :], xc[:, :]).then_inc(xT_written[half], 16)
                act.dma_start(to[F:XR, :], xc[0:XR - F, :]).then_inc(xT_written[half], 16)

            def relu(dst, src, bias, done):
                nc.scalar.activation(dst, src, ACT.Relu, bias=bias).then_inc(done, 1)

            def take0(s, cur, first=False):
                relu(h1[0:H, :], cur[0:H, :], bias0[0:H, :], read0)
                relu(h1[H:P, :], cur[0:H, :], bias0[0:H, :], read0)

            def direct0(s, cur, first=False):
                if not first:
                    act.wait_ge(sum_done, 2 * s - 1)
                relu(direct[H:P, :], cur[H:P, :], bias0[H:P, :], read0)

            def take1(cur):
                relu(h2[0:H, :], cur[H:P, :], bias1[H:P, :], read1)
                relu(h2[H:P, :], cur[H:P, :], bias1[H:P, :], read1)

            def direct1(cur, b=None):
                if b is not None:
                    act.wait_ge(xT_written[1], 32 * (b + 1))
                relu(direct[0:H, :], cur[0:H, :], bias1[0:H, :], read1)

            def take2(cur):
                relu(cur[:, :], cur[:, :], bias2[:, :], read2)

            copy_xc(0, 0, curA, first=True)
            copy_xc(0, 1, curB)
            act.wait_ge(small_loaded, 16 * 7)
            for i in range(-HEAD, 0):
                hi(PAIR_KINDS, 0, i)
                if i == -T1 - 1:
                    act.wait_ge(z_used, T0)
                    take0(0, curA, first=True)
                    direct0(0, curA, first=True)

            def round_(kinds, s, j, i0, cur, other, b_next, b_xc):
                for u in range(ROUND):
                    i = i0 + u
                    hi(kinds, j, i)
                    if u == LAG_READ - 1:
                        act.wait_ge(z_used, start(j) + i0)
                        take1(other)
                    if u == LAG_READ - 1 + LAG_DIRECT:
                        direct1(other, b_xc)
                    if u == T0 - 1 + LAG_READ:
                        act.wait_ge(z_used, start(j) + i0 + T0)
                        take0(s + 1, cur)
                    if u == T0 - 1 + LAG_READ + LAG_DIRECT:
                        direct0(s + 1, cur)
                    if b_next is not None and u in (T0 + 7, T0 + 13):
                        copy_xc(b_next, int(u == T0 + 13), cur)
                    if b_xc is None and u == T0 + T1 + 7:
                        act.wait_ge(dense_turned, 1)
                        nc.scalar.activation(zC, h2[0:DN, :], ACT.Copy).then_inc(dense_copied, 1)
                    if u == T0 + T1 - 1 + LAG_READ:
                        act.wait_ge(z_used, start(j) + i0 + T0 + T1)
                        take2(other)

            with act.Fori(0, NB - 1) as j:
                round_(PAIR_KINDS, 2 * j, j, 0, curA, curB, j + 1, j)
                round_(PAIR_KINDS, 2 * j + 1, j, ROUND, curB, curA, None, j + 1)
            j = NB - 1
            round_(LAST_KINDS, NST - 2, j, 0, curA, curB, None, None)
            act.wait_ge(z_used, start(j) + ROUND)
            take1(curA)
            direct1(curA)

            def read_top(g):
                layer, n, m, cur, cols = GROUPS[g]
                act.wait_ge(top_done, g + 1)
                if layer == 1:
                    relu(hid1[n][m], cur[:, cols], bt1[:, m:m + 1], top_read)
                elif layer == 2:
                    relu(hid2[n][m], cur[:, cols], bt2[:, m:m + 1], top_read)
                else:
                    nc.scalar.activation(y[:, n * BK:(n + 1) * BK], cur[0:1, cols], ACT.Copy).then_inc(top_read, 1)

            for i in range(ROUND, ROUND + T1):
                hi(LAST_KINDS, j, i)
                if i == ROUND + 2:
                    read_top(0)
                    read_top(1)
                if i == ROUND + 6:
                    read_top(2)
                    read_top(3)
            act.wait_ge(z_used, start(j) + ROUND + T1)
            take2(curA)
            for g in range(EARLY, len(GROUPS)):
                read_top(g)

        @block.tensor
        def _(pe):
            def transposes(half, cur):
                ev = emb[:, :].rearrange("p (f d) -> p f d", d=D)
                for r in range(2):
                    for c in range(4):
                        mm = nc.tensor.transpose(cur[0:F, r * BK + c * P:r * BK + (c + 1) * P],
                                                 ev[:, :, HD * half + 4 * r + c], ident[:, :])
                    mm.then_inc(transposed, 1)

            def contract(kinds, j, i, cur, tiles):
                n, t = which_tile(kinds, i)
                r = R0 if n == 0 else rows1(t)
                first, stop = t == 0, t == tiles - 1

                def passes(w, v, start_, stop_):
                    for b in range(NBK):
                        mm = nc.tensor.matmul(cur[:, b * BK:(b + 1) * BK], w[0:r, :], v[0:r, b * BK:(b + 1) * BK],
                                              start=start_, stop=stop_)
                    return mm

                if kind(kinds, i) == "F":
                    pe.wait_ge(z_ready, start(j) + i + 1)
                    w = wf[n][:, full_at(n, t), :]
                    if n > 0 and stop:
                        for b in range(NBK):
                            p = slice(b * H, b * H + H)
                            mm = nc.tensor.matmul(cur[:, b * BK:(b + 1) * BK], w[p, :], z[p, slot(i), 0:BK],
                                                  start=False, stop=True)
                    else:
                        mm = passes(w, z[:, slot(i), :], first, stop)
                else:
                    h, q = split_slot(kinds, i, HI_RING), split_slot(kinds, i, LO_RING)
                    w = split_at(n, t)
                    pe.wait_ge(hi_ready, total("DG", j) + splits(kinds, i))
                    passes(wl[n][:, w, :], zh[:, h, :], first, False)
                    passes(wh[n][:, w, :], zh[:, h, :], False, False)
                    lo = lo_dve if kind(kinds, i) == "D" else lo_pool
                    pe.wait_ge(lo, total(kind(kinds, i), j) + splits(kinds, i, kind(kinds, i)))
                    mm = passes(wh[n][:, w, :], zl[:, q, :], False, stop)
                mm.then_inc(z_used, 1)

            pe.wait_ge(ident_ready, 1)
            pe.wait_ge(gathered, 16 * F)
            transposes(0, curA)
            transposes(1, curB)
            pe.wait_ge(w_hi, sum(len(k) for k in KINDS.values()))
            pe.wait_ge(w_lo, sum(len(k) - k.count("F") for k in KINDS.values()))
            pe.wait_ge(xc_copied, 4)
            for i in range(-HEAD, 0):
                if i < -T1:
                    contract(PAIR_KINDS, 0, i, curA, T0)
                else:
                    contract(PAIR_KINDS, 0, i, curB, T1)

            def round_(kinds, s, j, i0, cur, other, b_next, last=False):
                for u in range(T0):
                    contract(kinds, j, i0 + u, cur, T0)
                pe.wait_ge(read1, 3 * (s + 1))
                for u in range(T0, T0 + T1):
                    contract(kinds, j, i0 + u, other, T1)
                    if b_next is not None and u == T0 + 4:
                        pe.wait_ge(read0, 3 * (s + 2))
                        pe.wait_ge(gathered, 16 * F * (b_next + 1))
                        pe.nop(nofuse=True)
                        transposes(0, cur)
                    if b_next is not None and u == T0 + 10:
                        pe.wait_ge(xc_copied, 4 * b_next + 2)
                        pe.nop(nofuse=True)
                        transposes(1, cur)
                pe.wait_ge(read0, 3 * (s + 2))
                if b_next is not None:
                    pe.wait_ge(xc_copied, 4 * b_next + 4)
                for u in range(T0 + T1, ROUND):
                    contract(kinds, j, i0 + u, cur, T1)
                    if last and u == T0 + T1 + 4:
                        pe.wait_ge(dense_loaded, 16)
                        for c in range(NB):
                            mm = nc.tensor.transpose(h2[0:DN, c * P:(c + 1) * P], dn[:, c, :], ident[:, :])
                        mm.then_inc(dense_turned, 1)

            with pe.Fori(0, NB - 1) as j:
                round_(PAIR_KINDS, 2 * j, j, 0, curA, curB, j + 1)
                round_(PAIR_KINDS, 2 * j + 1, j, ROUND, curB, curA, None)
            j = NB - 1
            round_(LAST_KINDS, NST - 2, j, 0, curA, curB, None, last=True)

            def top(g):
                layer, n, m, cur, cols = GROUPS[g]
                users = [q for q in range(g) if GROUPS[q][3] is cur and GROUPS[q][4] == cols]
                need = [users[-1] + 1] if users else []
                if layer > 1:
                    need.append(groups_before(layer - 1, n))
                if need:
                    pe.wait_ge(top_read, max(need))
                if layer == 1:
                    mc = slice(m * P, m * P + P)
                    parts = [(wA[:, mc], zAB[n][:, 0, :]), (wB[:, mc], zAB[n][:, 1, :]),
                             (wC[:, mc], zC[:, n * BK:(n + 1) * BK])]
                elif layer == 2:
                    parts = [(wt2[:, q, m * P:m * P + P], hid1[n][q]) for q in range(M1 // P)]
                else:
                    parts = [(wt3[:, q:q + 1], hid2[n][q]) for q in range(M2 // P)]
                for q, (w, v) in enumerate(parts):
                    mm = nc.tensor.matmul(cur[0:w.shape[1], cols], w, v, start=(q == 0), stop=(q == len(parts) - 1))
                mm.then_inc(top_done, 1)

            pe.wait_ge(top_loaded, 16 * 6)
            pe.wait_ge(dense_copied, 1)
            pe.wait_ge(sum_done, 2 * NST - 2)
            for g in range(EARLY):
                top(g)
            pe.wait_ge(read1, 3 * NST)
            for i in range(ROUND, ROUND + T1):
                contract(LAST_KINDS, j, i, curA, T1)
            pe.wait_ge(top2_loaded, 16 * 3)
            for g in range(EARLY, len(GROUPS)):
                if GROUPS[g][0:3] == (1, 1, 0):
                    pe.wait_ge(add_done, 2 * NB)
                if GROUPS[g][0:3] == (2, 1, 0):
                    pe.wait_ge(sum_done, 2 * NST)
                top(g)


_TBL = [f"tbl_{f}" for f in range(F)]
_INS = (["dense_ctx", "ids"] + _TBL + ["W_top1", "b_top1", "W_top2", "b_top2", "W_top3"]
        + ["L0_rec_W0", "L0_rec_W1", "L0_rec_W2", "L0_rec_b0", "L0_rec_b1", "L0_rec_b2"])


def kernel(**inputs):
    import numpy as _np
    import concourse.bacc as _bacc
    from concourse import mybir as _mybir
    from concourse.bass_utils import run_bass_kernel_spmd as _run

    nc = _bacc.Bacc("TRN2", target_bir_lowering=False, num_devices=1)
    arrays, aps = {}, {}
    for name in _INS:
        a = _np.ascontiguousarray(inputs[name])
        arrays[f"in_{name}_dram"] = a
        aps[name] = nc.dram_tensor(f"in_{name}_dram", a.shape, _mybir.dt.from_np(a.dtype), kind="ExternalInput").ap()
    out = nc.dram_tensor("out_0_dram", (B, 1), F32, kind="ExternalOutput").ap()
    args = [aps["dense_ctx"], aps["ids"], [aps[n] for n in _TBL]] + [aps[n] for n in _INS[2 + F:]]
    cin_tower(nc, *args, out)
    r = _run(nc, [arrays], core_ids=[0])
    return r.results[0]["out_0_dram"]
```
